# Optimizing a Trainium2 kernel written in Bass

```python
import numpy as np
import jax
import jax.numpy as jnp

def _softmax(x, axis=-1):
    return jax.nn.softmax(x, axis=axis)

def _gelu(x):
    return jax.nn.gelu(x, approximate=True)

def _silu(x):
    return jax.nn.silu(x)

def _sigmoid(x):
    return jax.nn.sigmoid(x)

def _layernorm(x, axis=-1, eps=1e-05):
    m = jnp.mean(x, axis=axis, keepdims=True)
    v = jnp.var(x, axis=axis, keepdims=True)
    return (x - m) / jnp.sqrt(v + eps)

def _scatter_add(tgt, idx, src, axis=0):
    return tgt.at[idx].add(src)

def _segment_sum(src, seg, n):
    return jax.ops.segment_sum(src, seg, n)
kernel_name = 'mk_seq_postln_d1_jaxref_r8_f9c096'

def setup_inputs(seed: int=0):
    np.random.seed(seed)
    _w = jnp.asarray

    def _L0_attn_setup():
        import jax, jax.numpy as jnp
        import numpy as np
        import math
        D_MODEL = 256
        D_STATE = 16
        EXPAND = 2
        D_INNER = D_MODEL * EXPAND
        DT_RANK = math.ceil(D_MODEL / 16)
        BATCH, SEQ_LEN = (2, 64)
        key = jax.random.key(seed)
        ks = jax.random.split(key, 6)
        x = jax.random.normal(ks[0], (BATCH, SEQ_LEN, D_INNER), dtype=jnp.float32)
        A_log = jnp.log(jax.random.uniform(ks[1], (D_INNER, D_STATE), minval=0.5, maxval=16.0, dtype=jnp.float32))
        D = jnp.ones((D_INNER,), dtype=jnp.float32)
        x_proj_w = 0.02 * jax.random.normal(ks[2], (DT_RANK + 2 * D_STATE, D_INNER), dtype=jnp.float32)
        dt_init_std = DT_RANK ** (-0.5)
        dt_proj_w = jax.random.uniform(ks[3], (D_INNER, DT_RANK), minval=-dt_init_std, maxval=dt_init_std, dtype=jnp.float32)
        dt = jnp.exp(jax.random.uniform(ks[4], (D_INNER,), dtype=jnp.float32) * (math.log(0.1) - math.log(0.001)) + math.log(0.001))
        dt = jnp.clip(dt, 0.0001, None)
        dt_proj_b = dt + jnp.log(-jnp.expm1(-dt))
        return {'x': x, 'A_log': A_log, 'D': D, 'x_proj_w': x_proj_w, 'dt_proj_w': dt_proj_w, 'dt_proj_b': dt_proj_b}
    _L0_attn_in = _L0_attn_setup()

    def _L0_ffn_setup():
        import jax, jax.numpy as jnp
        import numpy as np
        HIDDEN = 512
        INTER = 1792
        B, S = (4, 256)

        def _dequant_linear(x, wq, scale):
            w = wq.astype(x.dtype) * scale[:, None]
            return jnp.einsum('bsh,oh->bso', x, w)
        key = jax.random.key(seed)
        kx, kg, kgs, ku, kus, kd, kds = jax.random.split(key, 7)
        x = jax.random.normal(kx, (B, S, HIDDEN), dtype=jnp.float32)
        gate_wq = jax.random.randint(kg, (INTER, HIDDEN), -128, 128, dtype=jnp.int32)
        up_wq = jax.random.randint(ku, (INTER, HIDDEN), -128, 128, dtype=jnp.int32)
        down_wq = jax.random.randint(kd, (HIDDEN, INTER), -128, 128, dtype=jnp.int32)
        gate_scale = jax.random.uniform(kgs, (INTER,), dtype=jnp.float32) * 0.01 + 0.0001
        up_scale = jax.random.uniform(kus, (INTER,), dtype=jnp.float32) * 0.01 + 0.0001
        down_scale = jax.random.uniform(kds, (HIDDEN,), dtype=jnp.float32) * 0.01 + 0.0001
        return {'x': x, 'gate_wq': gate_wq, 'gate_scale': gate_scale, 'up_wq': up_wq, 'up_scale': up_scale, 'down_wq': down_wq, 'down_scale': down_scale}
    _L0_ffn_in = _L0_ffn_setup()
    _d = {'L0_attn_x': _L0_attn_in['x'], 'L0_attn_A_log': _L0_attn_in['A_log'], 'L0_attn_D': _L0_attn_in['D'], 'L0_attn_x_proj_w': _L0_attn_in['x_proj_w'], 'L0_attn_dt_proj_w': _L0_attn_in['dt_proj_w'], 'L0_attn_dt_proj_b': _L0_attn_in['dt_proj_b'], 'L0_ffn_gate_wq': _L0_ffn_in['gate_wq'], 'L0_ffn_gate_scale': _L0_ffn_in['gate_scale'], 'L0_ffn_up_wq': _L0_ffn_in['up_wq'], 'L0_ffn_up_scale': _L0_ffn_in['up_scale'], 'L0_ffn_down_wq': _L0_ffn_in['down_wq'], 'L0_ffn_down_scale': _L0_ffn_in['down_scale']}
    _x0 = _d['L0_attn_x']
    _d['L0_attn_x'] = jax.random.normal(jax.random.fold_in(jax.random.key(seed), 1), (4, 512, 512), dtype=_x0.dtype)
    del _x0
    return _d

def reference(L0_attn_x, L0_attn_A_log, L0_attn_D, L0_attn_x_proj_w, L0_attn_dt_proj_w, L0_attn_dt_proj_b, L0_ffn_gate_wq, L0_ffn_gate_scale, L0_ffn_up_wq, L0_ffn_up_scale, L0_ffn_down_wq, L0_ffn_down_scale):

    def _L0_attn_ref(x, A_log, D, x_proj_w, dt_proj_w, dt_proj_b):
        import jax, jax.numpy as jnp
        import numpy as np
        import math
        D_MODEL = 256
        D_STATE = 16
        EXPAND = 2
        D_INNER = D_MODEL * EXPAND
        DT_RANK = math.ceil(D_MODEL / 16)
        BATCH, SEQ_LEN = (2, 64)
        A = -jnp.exp(A_log)
        xp = jnp.einsum('bld,rd->blr', x, x_proj_w)
        dt_in = xp[..., :DT_RANK]
        B = xp[..., DT_RANK:DT_RANK + D_STATE]
        C = xp[..., DT_RANK + D_STATE:]
        dt = jax.nn.softplus(jnp.einsum('blr,dr->bld', dt_in, dt_proj_w) + dt_proj_b)
        dA = jnp.exp(dt[..., None] * A)
        dBx = dt[..., None] * B[:, :, None, :] * x[..., None]

        def step(h, inp):
            dA_t, dBx_t, C_t = inp
            h = dA_t * h + dBx_t
            y = jnp.einsum('bdn,bn->bd', h, C_t)
            return (h, y)
        h0 = jnp.zeros((x.shape[0], D_INNER, D_STATE), dtype=x.dtype)
        _, ys = jax.lax.scan(step, h0, (jnp.moveaxis(dA, 1, 0), jnp.moveaxis(dBx, 1, 0), jnp.moveaxis(C, 1, 0)))
        y = jnp.moveaxis(ys, 0, 1) + D * x
        return y

    def _L0_ffn_ref(x, gate_wq, gate_scale, up_wq, up_scale, down_wq, down_scale):
        import jax, jax.numpy as jnp
        import numpy as np
        HIDDEN = 512
        INTER = 1792
        B, S = (4, 256)

        def _dequant_linear(x, wq, scale):
            w = wq.astype(x.dtype) * scale[:, None]
            return jnp.einsum('bsh,oh->bso', x, w)
        g = _dequant_linear(x, gate_wq, gate_scale)
        u = _dequant_linear(x, up_wq, up_scale)
        h = jax.nn.silu(g) * u
        return _dequant_linear(h, down_wq, down_scale)
    x = L0_attn_x
    x = _layernorm(x + _L0_attn_ref(x, L0_attn_A_log, L0_attn_D, L0_attn_x_proj_w, L0_attn_dt_proj_w, L0_attn_dt_proj_b), axis=-1)
    x = _layernorm(x + _L0_ffn_ref(x, L0_ffn_gate_wq, L0_ffn_gate_scale, L0_ffn_up_wq, L0_ffn_up_scale, L0_ffn_down_wq, L0_ffn_down_scale), axis=-1)
    return x

_drawn_inputs = setup_inputs


def setup_inputs(seed=0):
    import zlib

    import numpy as np

    out = dict(_drawn_inputs(seed))
    spreads = {'L0_attn_D': (1.0, 0.2)}
    factors = {'L0_attn_A_log': 3.382, 'L0_attn_dt_proj_w': 6.695}
    for name, (base, spread) in spreads.items():
        noise = np.random.default_rng([zlib.crc32(name.encode()), seed]).standard_normal(out[name].shape)
        drawn = base * np.exp(spread * noise) if base else spread * noise
        out[name] = jnp.asarray(drawn.astype(out[name].dtype))
    for name, factor in factors.items():
        out[name] = (out[name] * factor).astype(out[name].dtype)
    return out
```

```python
import concourse.bass as bass
from concourse import mybir
from contextlib import ExitStack

P = 128
BATCH, SEQ, D = 4, 512, 512
TC, KC = SEQ // P, D // P
NS, RK = 16, 16
XR = RK + 2 * NS
INTER = 1792
OT = INTER // P
SLOTS = NS
EPS = 1e-5
X_UP = 2048.0
W_MAX = 128.0
H_BOUND = (1.02 * D * W_MAX) ** 2
H_TOP = 60000.0

fp32, fp16, i32 = mybir.dt.float32, mybir.dt.float16, mybir.dt.int32
ALU = mybir.AluOpType
ACT = mybir.ActivationFunctionType
AXX = mybir.AxisListType.X
ds = bass.ds


def build(nc, x, x_chan, A_log, Dw, xproj, dtw, dt_b, wg, gs, wu, us, wd, dscale, identity, out):
    ctx = ExitStack()
    with ctx:
        def sb(name, shape, dt=fp32):
            return ctx.enter_context(nc.sbuf_tensor(name, shape, dt))

        def sem(name):
            return ctx.enter_context(nc.semaphore(name))

        ident = sb("ident", [P, P])
        A = sb("A", [P, KC, NS])
        D1 = sb("D1", [P, D])
        ds_bc = sb("ds_bc", [P, D])
        xw = sb("xw", [P, KC, XR])
        dtw_sb = sb("dtw_sb", [RK + 1, D])
        gs_sb = sb("gs_sb", [P, OT])
        us_sb = sb("us_sb", [P, OT])
        small = sb("small", [P, 8])
        gu = sb("gu", [P, OT])
        neg_half = sb("neg_half", [P, TC])
        wg16 = sb("wg16", [P, KC, INTER], fp16)
        wu16 = sb("wu16", [P, KC, INTER], fp16)
        wd16 = sb("wd16", [P, OT, D], fp16)
        x_tok = sb("x_tok", [P, TC, D])
        ybuf = sb("ybuf", [P, TC, D])
        bc_next = sb("bc_next", [P, TC, XR])
        B_cur = sb("B_cur", [P, TC, NS])
        C_cur = sb("C_cur", [P, TC, NS])
        bcol = sb("bcol", [P, 2, TC])
        dt_tok = sb("dt_tok", [P, TC, D])
        dt_next = sb("dt_next", [P, KC, SEQ])
        dt_chan = sb("dt_chan", [P, KC, SEQ])
        u_tok = sb("u_tok", [P, TC, D])
        acc = sb("acc", [P, TC, D])
        x2 = sb("x2", [P, TC, D])
        st = sb("st", [P, TC, 6])
        mv = sb("mv", [P, TC, 2])
        rstd = sb("rstd", [P, TC])
        st2 = sb("st2", [P, 6])
        mv2 = sb("mv2", [P, 2])
        ve2 = sb("ve2", [P, TC])
        nm2 = sb("nm2", [P, TC])
        rstd2 = sb("rstd2", [P, TC])
        nmr2 = sb("nmr2", [P, TC])
        v = sb("v", [P, 2, TC, D])
        dA = sb("dA", [P, 2, KC, SEQ])
        h = sb("h", [P, 2, KC, SEQ])
        xh = sb("xh", [P, KC, SEQ], fp16)
        xl = sb("xl", [P, KC, SEQ], fp16)
        sh = sb("sh", [P, 4, SEQ])
        hp = sb("hp", [P, 2, OT, SEQ], fp16)
        stage = hp[:].rearrange("p a b c -> p (a b c)").bitcast(i32)
        ln_w = sh
        dtin = sh[0:RK + 1, 0, :]
        xp = sh[0:XR, 1, :]

        V = [ctx.enter_context(nc.psum_tensor(f"psV{i}", [P, SEQ], fp32)) for i in range(2)]
        H = [ctx.enter_context(nc.psum_tensor(f"psH{i}", [P, D], fp32)) for i in range(2)]
        F = ctx.enter_context(nc.psum_tensor("psF", [P, 4, 512], fp32))

        def sems(*names):
            return [sem(n) for n in names]

        const_in, scale_in, x_in, xc_in, al_in, out_done = sems(
            "const_in", "scale_in", "x_in", "xc_in", "al_in", "out_done")
        ones_set, A_exp, A_set, D1_set, nh_set = sems("ones_set", "A_exp", "A_set", "D1_set", "nh_set")
        c_gu, c_sq, c_par, c_all, c_pow, c_set, c_inv, scales_set = sems(
            "c_gu", "c_sq", "c_par", "c_all", "c_pow", "c_set", "c_inv", "scales_set")
        went_on = sem("went_on")
        w_conv = sem("w_conv")
        v_ready, V_done, dA_ready, scan_done, H_done, acc_done = sems(
            "v_ready", "V_done", "dA_ready", "scan_done", "H_done", "acc_done")
        bcol_set = sem("bcol_set")
        xp_ps, xp_set, bc_ps, bc_set, z_ps, z_abs, z_max, e_set, w1_set, r_set, ln_set, sp_set, dt_set = sems(
            "xp_ps", "xp_set", "bc_ps", "bc_set", "z_ps", "z_abs", "z_max", "e_set", "w1_set", "r_set", "ln_set",
            "sp_set", "dt_set")
        dtc_ps, dtc_next, dtc_cur, u_set, B_set, C_set, acc_init = sems(
            "dtc_ps", "dtc_next", "dtc_cur", "u_set", "B_set", "C_set", "acc_init")
        ln1_st, ln1_mv, ln1_ve, ln1_rstd, x2_set, x2T_ps, xh_set, xl_set = sems(
            "ln1_st", "ln1_mv", "ln1_ve", "ln1_rstd", "x2_set", "x2T_ps", "xh_set", "xl_set")
        gate_ps, up_ps, silu_set, h_set, hh_set, hl_set = sems(
            "gate_ps", "up_ps", "silu_set", "h_set", "hh_set", "hl_set")
        down_ps, ds_done, y_set, ln2_st, ln2_mv, ln2_ve, ln2_rstd, ln2_nmr, out_set = sems(
            "down_ps", "ds_done", "y_set", "ln2_st", "ln2_mv", "ln2_ve", "ln2_rstd", "ln2_nmr", "out_set")

        block = ctx.enter_context(nc.Block())

        def wait(eng, s, value):
            if not isinstance(value, int) or value > 0:
                eng.wait_ge(s, value)

        def apart(eng):
            eng.sem_inc(went_on, 1)

        def w_chunks():
            for k in range(KC):
                yield wg[k * P:(k + 1) * P, :], wg16[:, k, :]
                yield wu[k * P:(k + 1) * P, :], wu16[:, k, :]
            for t0 in range(0, OT, 3):
                n = min(3, OT - t0)
                yield (wd.rearrange("(t p) d -> p t d", p=P)[:, t0:t0 + n, :],
                       wd16[:, t0:t0 + n, :])
        CH = list(w_chunks())
        CHW = INTER
        Z_BANK = (0, 2, 3, 1)
        NST = OT * SEQ // CHW
        stage_in = [sem(f"stage_in{i}") for i in range(NST)]

        def place(i, dst):
            if len(dst.shape) == 2:
                return stage[:, (i % NST) * CHW:(i % NST) * CHW + INTER]
            n = dst.shape[1]
            return stage[:, (i % NST) * CHW:(i % NST) * CHW + n * D].rearrange("p (t d) -> p t d", d=D)

        @block.sync
        def _(sp):
            sp.dma_start(ybuf[:], x_chan[0].rearrange("(k p) t -> p k t", p=P)).then_inc(xc_in, 16)
            sp.dma_start(xw[:], xproj.rearrange("(k p) r -> p k r", p=P)).then_inc(const_in, 16)
            sp.dma_start(ident[:], identity).then_inc(const_in, 16)
            sp.dma_start(dtw_sb[0:RK, :], dtw).then_inc(const_in, 16)
            sp.dma_start(dtw_sb[RK:RK + 1, :], dt_b).then_inc(const_in, 16)
            sp.dma_start(A[:], A_log.rearrange("(k p) n -> p k n", p=P)).then_inc(al_in, 16)
            sp.dma_start(x_tok[:], x[0].rearrange("(c p) d -> p c d", p=P)).then_inc(x_in, 16)
            sp.dma_start(D1[:], Dw.to_broadcast([P, D])).then_inc(scale_in, 16)
            sp.dma_start(ds_bc[:], dscale.to_broadcast([P, D])).then_inc(scale_in, 16)
            sp.dma_start(gs_sb[:], gs).then_inc(scale_in, 16)
            sp.dma_start(us_sb[:], us).then_inc(scale_in, 16)

            def load_weights(first, after):
                for i in range(first, after):
                    wait(sp, w_conv, i - NST + 1)
                    sp.dma_start(place(i, CH[i][1]), CH[i][0]).then_inc(stage_in[i % NST], 16)

            load_weights(0, NST)
            for r in range(BATCH + 1):
                if r < BATCH - 1:
                    sp.wait_ge(dt_set, r + 1)
                    wait(sp, out_done, 64 * (r - 1))
                    sp.dma_start(ybuf[:], x_chan[r + 1].rearrange("(k p) t -> p k t", p=P)).then_inc(xc_in, 16)
                    sp.wait_ge(u_set, r + 1)
                    sp.wait_ge(acc_init, r + 1)
                    sp.dma_start(x_tok[:], x[r + 1].rearrange("(c p) d -> p c d", p=P)).then_inc(x_in, 16)
                if r == 0:
                    load_weights(NST, len(CH))
                if r > 0:
                    with sp.Fori(0, TC) as c:
                        sp.wait_ge(out_set, c + (4 * (r - 1) + 1))
                        sp.dma_start(out[ds(c * P + (r - 1) * SEQ, P), :],
                                     ybuf[:, ds(c, 1), :].rearrange("p a d -> p (a d)")).then_inc(out_done, 16)
            sp.wait_ge(out_done, 64 * BATCH)

        @block.tensor
        def _(pe):
            def v_to_chan(r, s, par, j):
                if j == 0:
                    pe.wait_ge(v_ready, 64 * r + 4 * s + 4)
                wait(pe, scan_done, 64 * r + 4 * s + j - 1)
                for c in range(TC):
                    last = nc.tensor.transpose(V[j % 2][:, c * P:(c + 1) * P], v[:, par, c, j * P:(j + 1) * P], ident[:])
                last.then_inc(V_done, 1)

            def h_to_tok(r, s, par, c):
                if c == 0:
                    pe.wait_ge(scan_done, 64 * r + 4 * s)
                wait(pe, acc_done, 64 * r + 4 * s - 5 + c)
                for k in range(KC):
                    last = nc.tensor.transpose(H[c % 2][:, k * P:(k + 1) * P], h[:, 1 - par, k, c * P:(c + 1) * P], ident[:])
                last.then_inc(H_done, 1)

            def slot(r, s, par, work=(None,) * 4, scans=True, before=True):
                for j in range(4):
                    if scans:
                        v_to_chan(r, s, par, j)
                    if before:
                        h_to_tok(r, s, par, j)
                    if work[j]:
                        work[j]()

            def product(w16, bank, t, done):
                for k in range(KC):
                    for i, part in enumerate((xh, xl)):
                        last = nc.tensor.matmul(F[:, bank, :], w16[:, k, ds(t * P, P)], part[:, k, :],
                                                start=(k == 0 and i == 0), stop=(k == KC - 1 and i == 1))
                last.then_inc(done, 1)

            def gate(r, t, q, first=False):
                if first:
                    pe.wait_ge(xh_set, 4 * r)
                    pe.wait_ge(xl_set, 4 * r)
                else:
                    pe.wait_ge(silu_set, OT * (r - 1) + t - 1)
                product(wg16, q, t, gate_ps)

            def up(r, t, q, first=False):
                if not first:
                    pe.wait_ge(h_set, OT * (r - 1) + t - 1)
                product(wu16, 2 + q, t, up_ps)

            def tiles(r, t):
                return [lambda: gate(r, t, 0), lambda: gate(r, t + 1, 1), lambda: up(r, t, 0), lambda: up(r, t + 1, 1)]

            def project(b, r):
                pe.wait_ge(xc_in, 16 * (b + 1))
                if r is None:
                    pe.wait_ge(const_in, 64)
                elif isinstance(r, int) and r == 0:
                    pe.wait_ge(dtc_next, 4)
                else:
                    pe.wait_ge(silu_set, OT * (r - 1) + 10)
                    pe.wait_ge(h_set, OT * (r - 1) + 10)
                for k in range(KC):
                    last = nc.tensor.matmul(F[0:XR, 0, :], xw[:, k, :], ybuf[:, k, :], start=(k == 0), stop=(k == KC - 1))
                last.then_inc(xp_ps, 1)
                pe.wait_ge(xp_set, b + 1)
                apart(pe)
                for c in range(TC):
                    last = nc.tensor.transpose(F[:, 1, c * XR:(c + 1) * XR], xp[:, c * P:(c + 1) * P], ident[0:XR, 0:XR])
                last.then_inc(bc_ps, 1)
                for c in range(TC):
                    if c == 3:
                        pe.wait_ge(bc_set, b + 1)
                    nc.tensor.matmul(F[:, Z_BANK[c], :], dtin[:, c * P:(c + 1) * P], dtw_sb[:, :],
                                     start=True, stop=True).then_inc(z_ps, 1)

            def dt_to_chan(b, r):
                pe.wait_ge(dt_set, b + 1)
                if r is not None and not (isinstance(r, int) and r == 0):
                    pe.wait_ge(silu_set, OT * r)
                    pe.wait_ge(h_set, OT * r)
                for k in range(KC):
                    for c in range(TC):
                        last = nc.tensor.transpose(F[:, k, c * P:(c + 1) * P], dt_tok[:, c, k * P:(k + 1) * P], ident[:])
                    last.then_inc(dtc_ps, 1)

            def x2_to_chan(r):
                pe.wait_ge(x2_set, 4 * r)
                if isinstance(r, int):
                    pe.wait_ge(dtc_next, min(4 * (r + 1), 4 * BATCH))
                else:
                    pe.wait_ge(dtc_next, 4 * r + 4)
                for k in range(KC):
                    for c in range(TC):
                        last = nc.tensor.transpose(F[:, k, c * P:(c + 1) * P], x2[:, c, k * P:(k + 1) * P], ident[:])
                    last.then_inc(x2T_ps, 1)

            def down(r, c, lot, setup):
                if lot == 0:
                    pe.wait_ge(hl_set, OT * r)
                    if setup:
                        pe.wait_ge(dtc_next, 4 * r + 5 + c)
                for i in range(28 * lot // 8, 28 * (lot + 1) // 8):
                    t, part = i // 2, i % 2
                    last = nc.tensor.matmul(F[:, ds(c, 1), :].rearrange("p a d -> p (a d)"), hp[:, part, t, ds(c * P, P)],
                                            wd16[:, t, :], start=(i == 0), stop=(i == 27))
                if lot == 7:
                    last.then_inc(down_ps, 1)

            def round_(r, scans=True, ffn=True, setup=True):
                slot(r, 0, 0, scans=scans, before=ffn)
                if scans:
                    slot(r, 1, 1)
                if ffn:
                    x2_to_chan(r)
                    pe.wait_ge(w_conv, len(CH))
                    gate(r, 0, 0, first=True)
                    gate(r, 1, 1, first=True)
                    up(r, 0, 0, first=True)
                    up(r, 1, 1, first=True)

                def two_slots(i):
                    for half in range(2):
                        work = tiles(r, 4 * i - 2 + 2 * half) if ffn else (None,) * 4
                        if scans:
                            slot(r, 2 * i + half, half, work)
                        else:
                            for part in work:
                                part()

                with pe.Fori(1, 3) as i:
                    two_slots(i)
                if setup:
                    project(r + 1, r)
                if setup and ffn:
                    pe.wait_ge(z_abs, 4 * r + 8)
                    pe.wait_ge(z_max, 4 * r + 8)
                two_slots(3)
                if setup:
                    dt_to_chan(r + 1, r)
                with pe.Fori(0, TC) as c:
                    for half in range(2):
                        work = [(lambda lot=4 * half + n: down(r, c, lot, setup)) if ffn else None for n in range(4)]
                        if scans:
                            slot(r, 2 * c + (8 + half), half, work)
                        else:
                            for part in work:
                                part()

            project(0, None)
            dt_to_chan(0, None)
            round_(0, ffn=False)
            with pe.Fori(1, BATCH - 1) as r:
                round_(r)
            round_(BATCH - 1, setup=False)
            round_(BATCH, scans=False, setup=False)

        @block.scalar
        def _(act):
            def exps(r, s, par):
                for j in range(KC):
                    wait(act, scan_done, 64 * r + 4 * s + j - 7)
                    nc.scalar.activation(dA[:, par, j, :], dt_chan[:, j, :], ACT.Exp,
                                         scale=A[:, j, ds(s, 1)]).then_inc(dA_ready, 1)

            def take_dt(r):
                act.wait_ge(dtc_next, 4 * r + 4)
                wait(act, dA_ready, 64 * r)
                nc.scalar.copy(dt_chan[:], dt_next[:]).then_inc(dtc_cur, 1)
                act.wait_ge(dtc_cur, r + 1)

            def project(b, r):
                act.wait_ge(xp_ps, b + 1)
                if r is not None and not (isinstance(r, int) and r == 0):
                    act.wait_ge(hl_set, OT * (r - 1) + 10)
                nc.scalar.activation(dtin, dtw_sb[:], ACT.Copy, bias=1.0, scale=0.0).then_inc(ones_set, 1)
                act.wait_ge(ones_set, b + 1)
                nc.scalar.copy(dtin[0:RK, :], F[0:RK, 0, :])
                nc.scalar.copy(xp, F[0:XR, 0, :]).then_inc(xp_set, 1)
                if r is not None:
                    act.wait_ge(B_set, b)
                    act.wait_ge(C_set, b)
                act.wait_ge(bc_ps, b + 1)
                nc.scalar.copy(bc_next[:].rearrange("p c n -> p (c n)"), F[:, 1, 0:TC * XR]).then_inc(bc_set, 1)
                for c in range(TC):
                    act.wait_ge(z_max, 4 * b + c + 1)
                    nc.scalar.activation(ybuf[:, c, :], F[:, Z_BANK[c], :], ACT.Abs).then_inc(z_abs, 1)
                act.wait_ge(z_abs, 4 * b + 4)
                nc.scalar.activation(ybuf[:], ybuf[:], ACT.Exp, scale=-1.0).then_inc(e_set, 1)
                act.wait_ge(e_set, b + 1)
                act.wait_ge(z_ps, 4 * b + 4)
                nc.scalar.activation(ln_w[:], ybuf[:], ACT.Ln, bias=1.0).then_inc(ln_set, 1)

            def dt_out(b):
                for k in range(KC):
                    act.wait_ge(dtc_ps, 4 * b + k + 1)
                    nc.scalar.copy(dt_next[:, k, :], F[:, k, :]).then_inc(dtc_next, 1)

            def high_x(r):
                for k in range(KC):
                    act.wait_ge(x2T_ps, 4 * (r - 1) + k + 1)
                    nc.scalar.activation(xh[:, k, :], F[:, k, :], ACT.Copy, scale=X_UP).then_inc(xh_set, 1)

            def tiles(r, t, first=False):
                for q in range(2):
                    act.wait_ge(gate_ps, OT * (r - 1) + t + (q + 1))
                    if not first:
                        act.wait_ge(h_set, OT * (r - 1) + t + (q - 1))
                    nc.scalar.activation(sh[:, q, :], F[:, q, :], ACT.Silu, scale=gs_sb[:, ds(t + q, 1)]).then_inc(silu_set, 1)
                for q in range(2):
                    act.wait_ge(h_set, OT * (r - 1) + t + (q + 1))
                    nc.scalar.copy(hp[:, 0, ds(t + q, 1), :].rearrange("p a t -> p (a t)"), sh[:, 2 + q, :]).then_inc(hh_set, 1)

            def norm2(r, c):
                act.wait_ge(ln2_nmr, 4 * (r - 1) + c + 1)
                y = ybuf[:, ds(c, 1), :].rearrange("p a d -> p (a d)")
                nc.scalar.activation(y, y, ACT.Identity, bias=nmr2[:, ds(c, 1)], scale=rstd2[:, ds(c, 1)]).then_inc(out_set, 1)

            def convert(i):
                act.wait_ge(stage_in[i % NST], 16 * (i // NST + 1))
                nc.scalar.copy(CH[i][1], place(i, CH[i][1])).then_inc(w_conv, 1)

            def round_(r, scans=True, ffn=True, setup=True, last3=True):
                if scans:
                    take_dt(r)
                    exps(r, 0, 0)
                    exps(r, 1, 1)
                if last3:
                    norm2(r - 1, 3)
                if ffn:
                    high_x(r)
                if scans:
                    exps(r, 2, 0)
                if ffn:
                    tiles(r, 0, first=True)
                with act.Fori(1, 3) as i:
                    for half in range(2):
                        if scans:
                            exps(r, 2 * i + (1 + half), 1 - half)
                        if ffn:
                            tiles(r, 4 * i + (2 * half - 2))
                if scans:
                    exps(r, 7, 1)
                if setup:
                    project(r + 1, r)
                if setup:
                    act.wait_ge(sp_set, r + 2)
                if ffn:
                    tiles(r, 10)
                if scans:
                    exps(r, 8, 0)
                if ffn:
                    tiles(r, 12)
                if scans:
                    exps(r, 9, 1)
                if setup:
                    dt_out(r + 1)
                with act.Fori(0, 3) as c:
                    if scans:
                        exps(r, 2 * c + 10, 0)
                        exps(r, 2 * c + 11, 1)
                    if ffn:
                        norm2(r, c)

            def round_0():
                take_dt(0)
                for s in range(SLOTS):
                    exps(0, s, s % 2)
                    if 1 <= s <= len(CH):
                        convert(s - 1)
                    if s == 7:
                        project(1, 0)
                    if s == 9:
                        dt_out(1)

            act.wait_ge(al_in, 16)
            nc.scalar.activation(A[:], A[:], ACT.Exp).then_inc(A_exp, 1)
            act.wait_ge(const_in, 64)
            project(0, None)
            dt_out(0)
            act.wait_ge(A_set, 1)
            round_0()
            act.wait_ge(scales_set, 1)
            round_(1, last3=False)
            with act.Fori(2, BATCH - 1) as r:
                round_(r)
            round_(BATCH - 1, setup=False)
            round_(BATCH, scans=False, setup=False)
            norm2(BATCH, 3)

        @block.gpsimd
        def _(pool):
            def v_slot(r, s, par):
                wait(pool, v_ready, 64 * r + 4 * s - 4)
                apart(pool)
                nc.gpsimd.tensor_copy(bcol[:, par, :], B_cur[:, :, ds(s, 1)].rearrange("p c a -> p (c a)")).then_inc(bcol_set, 1)
                pool.wait_ge(bcol_set, SLOTS * r + s + 1)
                wait(pool, V_done, 64 * r + 4 * s - 4)
                apart(pool)
                for c in range(TC):
                    nc.gpsimd.tensor_scalar(v[:, par, c, :], u_tok[:, c, :], bcol[:, par, c:c + 1], 1.0,
                                            ALU.mult, ALU.mult).then_inc(v_ready, 1)

            def take_row(r):
                pool.wait_ge(dt_set, r + 1)
                pool.wait_ge(x_in, 16 * r + 16)
                wait(pool, v_ready, 64 * r)
                nc.gpsimd.tensor_tensor(u_tok[:], dt_tok[:], x_tok[:], ALU.mult).then_inc(u_set, 1)
                pool.wait_ge(bc_set, r + 1)
                apart(pool)
                nc.gpsimd.tensor_copy(B_cur[:], bc_next[:, :, RK:RK + NS]).then_inc(B_set, 1)
                pool.wait_ge(u_set, r + 1)
                pool.wait_ge(B_set, r + 1)
                apart(pool)

            def rstd1(r):
                pool.wait_ge(ln1_ve, r)
                nc.gpsimd.tensor_tensor(rstd[:], mv[:, :, 1], neg_half[:], ALU.pow).then_inc(ln1_rstd, 1)

            def rstd_2(r, c):
                pool.wait_ge(ln2_ve, 4 * (r - 1) + c + 1)
                nc.gpsimd.tensor_tensor(rstd2[:, ds(c, 1)], ve2[:, ds(c, 1)], neg_half[:, 0:1], ALU.pow).then_inc(ln2_rstd, 1)
                pool.wait_ge(ln2_rstd, 4 * (r - 1) + c + 1)
                nc.gpsimd.tensor_tensor(nmr2[:, ds(c, 1)], nm2[:, ds(c, 1)], rstd2[:, ds(c, 1)], ALU.mult).then_inc(ln2_nmr, 1)

            def low_h(r, t):
                for q in range(2):
                    pool.wait_ge(hh_set, OT * (r - 1) + t + (q + 1))
                    nc.gpsimd.tensor_tensor(hp[:, 1, ds(t + q, 1), :].rearrange("p a t -> p (a t)"), sh[:, 2 + q, :],
                                            hp[:, 0, ds(t + q, 1), :].rearrange("p a t -> p (a t)"),
                                            ALU.subtract).then_inc(hl_set, 1)

            def round_(r, scans=True, ffn=True, last3=True):
                if scans:
                    take_row(r)
                    v_slot(r, 0, 0)
                    v_slot(r, 1, 1)
                if last3:
                    rstd_2(r - 1, 3)
                if ffn:
                    rstd1(r)
                if scans:
                    v_slot(r, 2, 0)
                if ffn:
                    low_h(r, 0)
                with pool.Fori(1, 3) as i:
                    for half in range(2):
                        if scans:
                            v_slot(r, 2 * i + (1 + half), 1 - half)
                        if ffn:
                            low_h(r, 4 * i + (2 * half - 2))
                if scans:
                    v_slot(r, 7, 1)
                if ffn:
                    low_h(r, 10)
                if scans:
                    v_slot(r, 8, 0)
                if ffn:
                    low_h(r, 12)
                if scans:
                    v_slot(r, 9, 1)
                with pool.Fori(0, 3) as c:
                    if scans:
                        v_slot(r, 2 * c + 10, 0)
                        v_slot(r, 2 * c + 11, 1)
                    if ffn:
                        rstd_2(r, c)

            nc.gpsimd.memset(neg_half[:], -0.5).then_inc(nh_set, 1)
            pool.wait_ge(nh_set, 1)
            pool.wait_ge(c_par, 1)
            nc.gpsimd.partition_all_reduce(small[:, 1:2], small[:, 0:1], P, bass.bass_isa.ReduceOp.max).then_inc(c_all, 1)
            pool.wait_ge(c_all, 1)
            nc.gpsimd.tensor_tensor(small[:, 2:3], small[:, 1:2], neg_half[:, 0:1], ALU.pow).then_inc(c_pow, 1)
            round_(0, ffn=False, last3=False)
            round_(1, last3=False)
            with pool.Fori(2, BATCH) as r:
                round_(r)
            round_(BATCH, scans=False)
            rstd_2(BATCH, 3)

        @block.vector
        def _(dve):
            def scan(r, s, par, j):
                wait(dve, V_done, 64 * r + 4 * s + j + 1)
                wait(dve, dA_ready, 64 * r + 4 * s + j + 1)
                if j == 0:
                    wait(dve, H_done, 64 * r + 4 * s - 4)
                nc.vector.tensor_tensor_scan(h[:, par, j, :], dA[:, par, j, :], V[j % 2][:], 0.0,
                                             ALU.mult, ALU.add).then_inc(scan_done, 1)

            def add(r, s, c, n):
                dve.wait_ge(H_done, 64 * r + 4 * s - 3 + c)
                wait(dve, acc_done, 64 * r + 4 * s - 7 + c)
                nc.vector.scalar_tensor_tensor(acc[:, c, :], H[c % 2][:], C_cur[:, c, ds(n, 1)], acc[:, c, :],
                                               ALU.mult, ALU.add).then_inc(acc_done, 1)

            def slot(r, s, par, scans=True, before=True):
                for j in range(4):
                    if scans:
                        scan(r, s, par, j)
                    if before:
                        add(r, s, j, (NS - 1) if isinstance(s, int) and s == 0 else s - 1)

            def ln1(r):
                dve.wait_ge(acc_done, 64 * r)
                for c in range(TC):
                    last = nc.vector.bn_stats(st[:, c, :], acc[:, c, :])
                last.then_inc(ln1_st, 1)
                dve.wait_ge(ln1_st, r)
                apart(dve)
                for c in range(TC):
                    last = nc.vector.bn_aggr(mv[:, c, :], st[:, c, :])
                last.then_inc(ln1_mv, 1)
                dve.wait_ge(ln1_mv, r)
                nc.vector.tensor_scalar(mv[:, :, 1], mv[:, :, 1], EPS, None, ALU.add).then_inc(ln1_ve, 1)
                dve.wait_ge(ln1_rstd, r)
                for c in range(TC):
                    nc.vector.tensor_scalar(x2[:, c, :], acc[:, c, :], mv[:, c, 0:1], rstd[:, c:c + 1],
                                            ALU.subtract, ALU.mult).then_inc(x2_set, 1)

            def start_row(r):
                dve.wait_ge(x_in, 16 * r + 16)
                dve.wait_ge(D1_set, 1)
                if not (isinstance(r, int) and r == 0):
                    dve.wait_ge(x2_set, 4 * r)
                nc.vector.tensor_tensor(acc[:], x_tok[:], D1[:].rearrange("p (a d) -> p a d", a=1).to_broadcast([P, TC, D]),
                                        ALU.mult).then_inc(acc_init, 1)
                dve.wait_ge(bc_set, r + 1)
                nc.vector.tensor_copy(C_cur[:], bc_next[:, :, RK + NS:XR]).then_inc(C_set, 1)
                dve.wait_ge(acc_init, r + 1)
                dve.wait_ge(C_set, r + 1)

            def z_maxes(b, r):
                if r is not None:
                    dve.wait_ge(dtc_ps, 4 * b)
                    dve.wait_ge(u_set, b)
                for c in range(TC):
                    dve.wait_ge(z_ps, 4 * b + c + 1)
                    nc.vector.tensor_scalar(dt_tok[:, c, :], F[:, Z_BANK[c], :], 0.0, None, ALU.max).then_inc(z_max, 1)

            def softplus(b, r):
                dve.wait_ge(e_set, b + 1)
                if r is not None:
                    dve.wait_ge(dtc_cur, b)
                nc.vector.tensor_scalar(dt_next[:], ybuf[:], 1.0, 1.0, ALU.add, ALU.subtract).then_inc(w1_set, 1)
                dve.wait_ge(w1_set, b + 1)
                nc.vector.tensor_tensor(dt_next[:], ybuf[:], dt_next[:], ALU.subtract).then_inc(r_set, 1)
                dve.wait_ge(r_set, b + 1)
                dve.wait_ge(ln_set, b + 1)
                nc.vector.tensor_tensor(dt_next[:], ln_w[:], dt_next[:], ALU.add).then_inc(sp_set, 1)
                dve.wait_ge(sp_set, b + 1)
                dve.wait_ge(z_max, 4 * b + 4)
                nc.vector.tensor_tensor(dt_tok[:], dt_tok[:], dt_next[:], ALU.add).then_inc(dt_set, 1)

            def low_x(r):
                for k in range(KC):
                    dve.wait_ge(xh_set, 4 * (r - 1) + k + 1)
                    nc.vector.scalar_tensor_tensor(xl[:, k, :], F[:, k, :], X_UP, xh[:, k, :],
                                                   ALU.mult, ALU.subtract).then_inc(xl_set, 1)

            def tiles(r, t, first=False):
                for q in range(2):
                    dve.wait_ge(up_ps, OT * (r - 1) + t + (q + 1))
                    dve.wait_ge(silu_set, OT * (r - 1) + t + (q + 1))
                    if not first:
                        dve.wait_ge(hl_set, OT * (r - 1) + t + (q - 1))
                    nc.vector.scalar_tensor_tensor(sh[:, 2 + q, :], F[:, 2 + q, :], us_sb[:, ds(t + q, 1)], sh[:, q, :],
                                                   ALU.mult, ALU.mult).then_inc(h_set, 1)

            def finish(r, c, free):
                n = 4 * (r - 1) + c + 1
                y = ybuf[:, ds(c, 1), :].rearrange("p a d -> p (a d)")
                dve.wait_ge(down_ps, n)
                if free:
                    dve.wait_ge(out_done, 64 * (r - 1))
                nc.vector.tensor_tensor(y, F[:, ds(c, 1), :].rearrange("p a d -> p (a d)"), ds_bc[:], ALU.mult).then_inc(ds_done, 1)
                dve.wait_ge(ds_done, n)
                nc.vector.tensor_tensor(y, y, x2[:, ds(c, 1), :].rearrange("p a d -> p (a d)"), ALU.add).then_inc(y_set, 1)
                dve.wait_ge(y_set, n)
                apart(dve)
                nc.vector.bn_stats(st2[:], y).then_inc(ln2_st, 1)
                dve.wait_ge(ln2_st, n)
                apart(dve)
                nc.vector.bn_aggr(mv2[:], st2[:]).then_inc(ln2_mv, 1)
                dve.wait_ge(ln2_mv, n)
                nc.vector.tensor_scalar(nm2[:, ds(c, 1)], mv2[:, 0:1], -1.0, None, ALU.mult)
                nc.vector.tensor_scalar(ve2[:, ds(c, 1)], mv2[:, 1:2], EPS, None, ALU.add).then_inc(ln2_ve, 1)
                dve.wait_ge(ln2_ve, n)

            def round_(r, scans=True, ffn=True, setup=True, free=False):
                slot(r, 0, 0, scans, ffn)
                if ffn:
                    ln1(r)
                if scans:
                    start_row(r)
                    slot(r, 1, 1)
                if ffn:
                    low_x(r)
                    tiles(r, 0, first=True)
                with dve.Fori(1, 3) as i:
                    for half in range(2):
                        if scans:
                            slot(r, 2 * i + half, half)
                        if ffn:
                            tiles(r, 4 * i + (2 * half - 2))
                if setup:
                    z_maxes(r + 1, r)
                if scans:
                    slot(r, 6, 0)
                if setup:
                    softplus(r + 1, r)
                if ffn:
                    tiles(r, 10)
                if scans:
                    slot(r, 7, 1)
                if ffn:
                    tiles(r, 12)
                with dve.Fori(0, TC) as c:
                    if scans:
                        slot(r, 2 * c + 8, 0)
                        slot(r, 2 * c + 9, 1)
                    if ffn:
                        finish(r, c, free)

            z_maxes(0, None)
            softplus(0, None)
            dve.wait_ge(A_exp, 1)
            nc.vector.tensor_scalar(A[:], A[:], -1.0, None, ALU.mult).then_inc(A_set, 1)
            dve.wait_ge(scale_in, 64)
            nc.vector.tensor_scalar(D1[:], D1[:], 1.0, None, ALU.add).then_inc(D1_set, 1)
            nc.vector.tensor_tensor(gu[:], gs_sb[:], us_sb[:], ALU.mult).then_inc(c_gu, 1)
            dve.wait_ge(c_gu, 1)
            nc.vector.tensor_tensor(gu[:], gu[:], gu[:], ALU.mult).then_inc(c_sq, 1)
            dve.wait_ge(c_sq, 1)
            nc.vector.reduce_max(small[:, 0:1], gu[:], AXX).then_inc(c_gu, 1)
            dve.wait_ge(c_gu, 2)
            nc.vector.tensor_scalar(small[:, 0:1], small[:, 0:1], 1e-30, None, ALU.max).then_inc(c_par, 1)
            dve.wait_ge(c_pow, 1)
            nc.vector.tensor_scalar(small[:, 3:4], small[:, 2:3], H_TOP / H_BOUND, None, ALU.mult).then_inc(c_set, 1)
            dve.wait_ge(c_set, 1)
            nc.vector.reciprocal(small[:, 4:5], small[:, 3:4]).then_inc(c_inv, 1)
            dve.wait_ge(c_inv, 1)
            nc.vector.tensor_scalar(ds_bc[:], ds_bc[:], small[:, 4:5], None, ALU.mult)
            nc.vector.tensor_scalar(us_sb[:], us_sb[:], small[:, 3:4], 1.0 / X_UP, ALU.mult, ALU.mult)
            nc.vector.tensor_scalar(gs_sb[:], gs_sb[:], 1.0 / X_UP, None, ALU.mult).then_inc(scales_set, 1)
            dve.wait_ge(scales_set, 1)
            round_(0, ffn=False)
            with dve.Fori(1, BATCH - 1) as r:
                round_(r)
            round_(BATCH - 1, setup=False, free=True)
            round_(BATCH, scans=False, setup=False, free=True)


def kernel(**inputs):
    import numpy as np
    import concourse.bacc as bacc
    from concourse.bass_utils import run_bass_kernel_spmd

    a = {k.replace("L0_attn_", "").replace("L0_ffn_", ""): np.asarray(val) for k, val in inputs.items()}

    def t_(w):
        return np.ascontiguousarray(w.T)

    arrays = {
        "x": np.ascontiguousarray(a["x"]),
        "x_chan": np.ascontiguousarray(a["x"].transpose(0, 2, 1)),
        "A_log": np.ascontiguousarray(a["A_log"]),
        "Dw": a["D"].reshape(1, -1),
        "xproj": t_(a["x_proj_w"]),
        "dtw": t_(a["dt_proj_w"]),
        "dt_b": a["dt_proj_b"].reshape(1, -1),
        "wg": t_(a["gate_wq"]),
        "gs": t_(a["gate_scale"].reshape(-1, 128)),
        "wu": t_(a["up_wq"]),
        "us": t_(a["up_scale"].reshape(-1, 128)),
        "wd": t_(a["down_wq"]),
        "dscale": a["down_scale"].reshape(1, -1),
        "identity": np.eye(128, dtype=np.float32),
    }
    nc = bacc.Bacc("TRN2", target_bir_lowering=False, num_devices=1)
    args = [nc.dram_tensor(f"in_{n}", v.shape, mybir.dt.from_np(v.dtype), kind="ExternalInput").ap()
            for n, v in arrays.items()]
    out = nc.dram_tensor("out_y", (BATCH * SEQ, D), fp32, kind="ExternalOutput").ap()
    build(nc, *args, out)
    r = run_bass_kernel_spmd(nc, [{f"in_{n}": v for n, v in arrays.items()}], core_ids=[0])
    return r.results[0]["out_y"].reshape(BATCH, SEQ, D)
```

```python
import concourse.bass as bass
from concourse import mybir
from contextlib import ExitStack

P = 128
BATCH, SEQ, D = 4, 512, 512
TC, KC = SEQ // P, D // P
NS, RK = 16, 16
XR = RK + 2 * NS
INTER = 1792
OT = INTER // P
SLOTS = NS
EPS = 1e-5
X_UP = 2048.0
W_MAX = 128.0
H_BOUND = (1.02 * D * W_MAX) ** 2
H_TOP = 60000.0

fp32, fp16, i32 = mybir.dt.float32, mybir.dt.float16, mybir.dt.int32
ALU = mybir.AluOpType
ACT = mybir.ActivationFunctionType
AXX = mybir.AxisListType.X
ds = bass.ds


def build(nc, x_d, xc_d, A_log, Dw, xproj, dtw, dt_b, wg, gs, wu, us, wd, dscale, identity, out):
    ctx = ExitStack()
    with ctx:
        def sb(name, shape, dt=fp32):
            return ctx.enter_context(nc.sbuf_tensor(name, shape, dt))

        def sem(name):
            return ctx.enter_context(nc.semaphore(name))

        ident = sb("ident", [P, P])
        A = sb("A", [P, KC, NS])
        D1 = sb("D1", [P, D])
        ds_bc = sb("ds_bc", [P, D])
        xw = sb("xw", [P, KC, XR])
        dtw_sb = sb("dtw_sb", [RK + 1, D])
        gs_sb = sb("gs_sb", [P, OT])
        us_sb = sb("us_sb", [P, OT])
        small = sb("small", [P, 5])
        gu = sb("gu", [P, OT])
        neg_half = sb("neg_half", [P, TC])
        wg16 = sb("wg16", [P, KC, INTER], fp16)
        wu16 = sb("wu16", [P, KC, INTER], fp16)
        wd16 = sb("wd16", [P, OT, D], fp16)
        x_tok = sb("x_tok", [P, TC, D])
        x_chan = sb("x_chan", [P, KC, SEQ])
        dt_chan = sb("dt_chan", [P, KC, SEQ])
        u_chan = sb("u_chan", [P, KC, SEQ])
        C_next = sb("C_next", [P, TC, NS])
        C_cur = sb("C_cur", [P, TC, NS])
        acc = sb("acc", [P, TC, D])
        x2 = sb("x2", [P, TC, D])
        ybuf = sb("ybuf", [P, TC, D])
        st = sb("st", [P, TC, 6])
        mv = sb("mv", [P, TC, 2])
        rstd = sb("rstd", [P, TC])
        st2 = sb("st2", [P, 6])
        mv2 = sb("mv2", [P, 2])
        ve2 = sb("ve2", [P, TC])
        nm2 = sb("nm2", [P, TC])
        rstd2 = sb("rstd2", [P, TC])
        nmr2 = sb("nmr2", [P, TC])
        Bb = sb("Bb", [P, 4, SEQ])
        dBx = sb("dBx", [P, 2, KC, SEQ])
        dA = sb("dA", [P, 2, KC, SEQ])
        h = sb("h", [P, 2, KC, SEQ])
        xh = sb("xh", [P, KC, SEQ], fp16)
        xl = sb("xl", [P, KC, SEQ], fp16)
        sh = sb("sh", [P, 4, SEQ])
        hp = sb("hp", [P, 2, OT, SEQ], fp16)
        stage = hp[:].rearrange("p a b c -> p (a b c)").bitcast(i32)
        dt_next = sh
        xh32 = xh[:].rearrange("p a b -> p (a b)").bitcast(fp32).rearrange("p (a b) -> p a b", a=2)
        xl32 = xl[:].rearrange("p a b -> p (a b)").bitcast(fp32).rearrange("p (a b) -> p a b", a=2)
        e_sp, t_sp = [xh32[:, 0, :], xl32[:, 0, :]], [xh32[:, 1, :], xl32[:, 1, :]]
        dtin = ybuf[0:RK + 1, 3, :]
        xp = ybuf[0:XR, 2, :]

        H = [ctx.enter_context(nc.psum_tensor(f"psH{i}", [P, D], fp32)) for i in range(2)]
        F = ctx.enter_context(nc.psum_tensor("psF", [P, 4, 512], fp32))
        G = [ctx.enter_context(nc.psum_tensor(f"psG{i}", [P, 512], fp32)) for i in range(2)]
        B_dram = nc.dram_tensor("B_rows", (2, NS, SEQ), fp32, kind="Internal").ap()

        def sems(*names):
            return [sem(n) for n in names]

        const_in, scale_in, x_in, xc_in, al_in, out_done, b_out = sems(
            "const_in", "scale_in", "x_in", "xc_in", "al_in", "out_done", "b_out")
        b_in = sems("b_in0", "b_in1", "b_in2", "b_in3")
        A_exp, A_set, D1_set, nh_set, zero_set = sems("A_exp", "A_set", "D1_set", "nh_set", "zero_set")
        c_gu, c_sq, c_max, c_par, c_all, c_pow, c_set, c_inv, scales_set = sems(
            "c_gu", "c_sq", "c_max", "c_par", "c_all", "c_pow", "c_set", "c_inv", "scales_set")
        went_on = sem("went_on")
        w_conv = sem("w_conv")
        dBx_ready, scan_done = sems("dBx_ready", "scan_done")
        dA_ready, H_done, acc_done = sems("dA_ready", "H_done", "acc_done")
        xp_ps, ones_set, xp_set, c_ps, cn_set, dt_cur, u_set, C_set, xd_set = sems(
            "xp_ps", "ones_set", "xp_set", "c_ps", "cn_set", "dt_cur", "u_set", "C_set", "xd_set")
        z_ps, z_abs, e_set, w1_set, r_set, ln_set, l_set, dt_set = sems(
            "z_ps", "z_abs", "e_set", "w1_set", "r_set", "ln_set", "l_set", "dt_set")
        ln1_st, ln1_mv, ln1_ve, ln1_rstd, x2_set, x2T_ps, xh_set, xl_set = sems(
            "ln1_st", "ln1_mv", "ln1_ve", "ln1_rstd", "x2_set", "x2T_ps", "xh_set", "xl_set")
        gate_ps, up_ps, silu_set, h_set, hh_set, hl_set = sems(
            "gate_ps", "up_ps", "silu_set", "h_set", "hh_set", "hl_set")
        down_ps, ds_done, y_set, ln2_st, ln2_mv, ln2_ve, ln2_rstd, ln2_nmr, out_set = sems(
            "down_ps", "ds_done", "y_set", "ln2_st", "ln2_mv", "ln2_ve", "ln2_rstd", "ln2_nmr", "out_set")

        block = ctx.enter_context(nc.Block())

        def wait(eng, s, value):
            if not isinstance(value, int) or value > 0:
                eng.wait_ge(s, value)

        def apart(eng):
            eng.sem_inc(went_on, 1)

        def w_chunks():
            for k in range(KC):
                yield wg[k * P:(k + 1) * P, :], wg16[:, k, :]
                yield wu[k * P:(k + 1) * P, :], wu16[:, k, :]
            for t0 in range(0, OT, 3):
                n = min(3, OT - t0)
                yield (wd.rearrange("(t p) d -> p t d", p=P)[:, t0:t0 + n, :],
                       wd16[:, t0:t0 + n, :])
        CH = list(w_chunks())
        CHW = INTER
        NST = OT * SEQ // CHW
        stage_in = [sem(f"stage_in{i}") for i in range(NST)]

        def place(i, dst):
            if len(dst.shape) == 2:
                return stage[:, (i % NST) * CHW:(i % NST) * CHW + INTER]
            n = dst.shape[1]
            return stage[:, (i % NST) * CHW:(i % NST) * CHW + n * D].rearrange("p (t d) -> p t d", d=D)

        DOWN_BY = (11, 13, 14, 15)
        DONE_BY = (13, 14, 15)

        def is_first(r):
            return isinstance(r, int) and r == 0

        @block.sync
        def _(sp):
            for k in range(KC):
                sp.dma_start(x_chan[:, k, :], xc_d[0, k * P:(k + 1) * P, :]).then_inc(xc_in, 16)
                if k == 0:
                    sp.dma_start(xw[:], xproj.rearrange("(k p) r -> p k r", p=P)).then_inc(const_in, 16)
            sp.dma_start(dtw_sb[0:RK, :], dtw).then_inc(const_in, 16)
            sp.dma_start(dtw_sb[RK:RK + 1, :], dt_b).then_inc(const_in, 16)
            sp.dma_start(ident[:], identity).then_inc(const_in, 16)
            sp.dma_start(A[:], A_log.rearrange("(k p) n -> p k n", p=P)).then_inc(al_in, 16)
            sp.dma_start(x_tok[:], x_d[0].rearrange("(c p) d -> p c d", p=P)).then_inc(x_in, 16)
            sp.dma_start(D1[:], Dw.to_broadcast([P, D])).then_inc(scale_in, 16)
            sp.dma_start(ds_bc[:], dscale.to_broadcast([P, D])).then_inc(scale_in, 16)
            sp.dma_start(gs_sb[:], gs).then_inc(scale_in, 16)
            sp.dma_start(us_sb[:], us).then_inc(scale_in, 16)

            def load_weights(i):
                if i < len(CH):
                    wait(sp, w_conv, i - NST + 1)
                    sp.dma_start(place(i, CH[i][1]), CH[i][0]).then_inc(stage_in[i % NST], 16)

            def rows_out(b, parity):
                sp.wait_ge(xp_set, b + 1)
                sp.dma_start(B_dram[parity], xp[RK + NS:XR, :]).then_inc(b_out, 16)

            def b_slot(r, s, parity, lane):
                wait(sp, dBx_ready, 16 * r + s - 3)
                sp.dma_start(Bb[:, lane, :], B_dram[parity, ds(s, 1), :].to_broadcast([P, SEQ])).then_inc(b_in[lane], 16)

            def four_slots(r, parity, first, weights=None):
                for n in range(4):
                    b_slot(r, first + n, parity, n)
                    if weights is not None:
                        load_weights(weights + n)

            rows_out(0, 0)
            sp.wait_ge(b_out, 16)
            for s in range(0, NS, 4):
                four_slots(0, 0, s, weights=s)
                if s == 8:
                    rows_out(1, 1)
            for r in range(1, BATCH):
                sp.wait_ge(b_out, 16 * (r + 1))
                with sp.Fori(0, 3) as i:
                    four_slots(r, r % 2, i * 4)
                if r + 1 < BATCH:
                    rows_out(r + 1, (r + 1) % 2)
                four_slots(r, r % 2, 12)
            sp.wait_ge(b_out, 16 * BATCH)

        @block.tensor
        def _(pe):
            def h_to_tok(r, s, par, c):
                if c == 0:
                    pe.wait_ge(scan_done, 16 * r + s)
                wait(pe, acc_done, 64 * r + 4 * s - 5 + c)
                for k in range(KC):
                    last = nc.tensor.transpose(H[c % 2][:, k * P:(k + 1) * P], h[:, 1 - par, k, c * P:(c + 1) * P], ident[:])
                last.then_inc(H_done, 1)

            def slot(r, s, par, work=(), before=True):
                for j in range(4):
                    if before:
                        h_to_tok(r, s, par, j)
                    if j < len(work):
                        work[j]()

            def product(w16, bank, t, done, x2_of=None):
                for k in range(KC):
                    if x2_of is not None:
                        pe.wait_ge(xh_set, 4 * (x2_of - 1) + k + 1)
                        pe.wait_ge(xl_set, 4 * (x2_of - 1) + k + 1)
                    for i, part in enumerate((xh, xl)):
                        last = nc.tensor.matmul(F[:, bank, :], w16[:, k, ds(t * P, P)], part[:, k, :],
                                                start=(k == 0 and i == 0), stop=(k == KC - 1 and i == 1))
                last.then_inc(done, 1)

            def gate(r, t, q, first=False):
                if not first:
                    pe.wait_ge(silu_set, OT * (r - 1) + t - 1)
                product(wg16, q, t, gate_ps, r if first and t == 0 else None)

            def up(r, t, q, first=False):
                if not first:
                    pe.wait_ge(h_set, OT * (r - 1) + t + 1)
                product(wu16, 2 + q, t, up_ps)

            def tiles(r, t):
                return [lambda: gate(r, t, 0), lambda: gate(r, t + 1, 1), lambda: up(r, t, 0), lambda: up(r, t + 1, 1)]

            def project_x(b):
                pe.wait_ge(xc_in, 64 * (b + 1))
                if is_first(b):
                    pe.wait_ge(const_in, 64)
                else:
                    pe.wait_ge(dt_set, 4 * b)
                for k in range(KC):
                    last = nc.tensor.matmul(G[0][0:XR, :], xw[:, k, :], x_chan[:, k, :], start=(k == 0), stop=(k == KC - 1))
                last.then_inc(xp_ps, 1)

            def c_to_tok(b):
                pe.wait_ge(xp_set, b + 1)
                apart(pe)
                for c in range(TC):
                    last = nc.tensor.transpose(G[1][:, c * 2 * NS:(c + 1) * 2 * NS], xp[0:2 * NS, c * P:(c + 1) * P],
                                               ident[0:2 * NS, 0:2 * NS])
                last.then_inc(c_ps, 1)

            def dt_raw(b, k):
                if k == 1:
                    pe.wait_ge(cn_set, b + 1)
                if k > 1:
                    pe.wait_ge(dt_set, 4 * b + k - 1)
                nc.tensor.matmul(G[k % 2][:], dtw_sb[:, k * P:(k + 1) * P], dtin, start=True, stop=True).then_inc(z_ps, 1)

            def x2_to_chan(r):
                pe.wait_ge(x2_set, 4 * r)
                for k in range(KC):
                    for c in range(TC):
                        last = nc.tensor.transpose(F[:, k, c * P:(c + 1) * P], x2[:, c, k * P:(k + 1) * P], ident[:])
                    last.then_inc(x2T_ps, 1)

            def down(r, first, after):
                for n in range(first, min(after, 4 * 2 * OT)):
                    c, i = n // (2 * OT), n % (2 * OT)
                    t, part = i % OT, i // OT
                    if n == 0:
                        pe.wait_ge(silu_set, OT * r)
                        pe.wait_ge(hh_set, OT * r - 2)
                    if n == OT - 2:
                        pe.wait_ge(hh_set, OT * r)
                    if n == OT:
                        pe.wait_ge(hl_set, OT * r + 2)
                    if n == 4 * OT:
                        pe.wait_ge(h_set, OT * r + 2)
                    last = nc.tensor.matmul(F[:, c, :], hp[:, part, t, c * P:(c + 1) * P], wd16[:, t, :],
                                            start=(i == 0), stop=(i == 27))
                    if i == 27:
                        last.then_inc(down_ps, 1)

            def round_(r, scans=True, ffn=True, setup=True):
                slot(r, 0, 0, before=ffn)
                if ffn:
                    if setup:
                        project_x(r + 1)
                    if scans:
                        h_to_tok(r, 1, 1, 0)
                        h_to_tok(r, 1, 1, 1)
                    if setup:
                        c_to_tok(r + 1)
                        dt_raw(r + 1, 0)
                    x2_to_chan(r)
                    pe.wait_ge(w_conv, len(CH))
                    gate(r, 0, 0, first=True)
                    if scans:
                        h_to_tok(r, 1, 1, 2)
                    gate(r, 1, 1, first=True)
                    if scans:
                        h_to_tok(r, 1, 1, 3)
                    up(r, 0, 0, first=True)
                    up(r, 1, 1, first=True)
                    if setup:
                        dt_raw(r + 1, 1)
                else:
                    slot(r, 1, 1)
                with pe.Fori(0, 2) as i:
                    work = tiles(r, 6 * i + 2) + tiles(r, 6 * i + 4) + tiles(r, 6 * i + 6) if ffn else []
                    for n in range(4):
                        slot(r, 4 * i + (2 + n), n % 2, work[3 * n:3 * n + 3], before=scans)
                if setup and not ffn:
                    project_x(r + 1)
                    c_to_tok(r + 1)
                    dt_raw(r + 1, 0)
                    dt_raw(r + 1, 1)
                for s in range(10, NS):
                    work = [lambda a=5 * (4 * (s - 10) + j): down(r, a, a + 5) for j in range(4)] if ffn else []
                    if setup and s in (12, 13):
                        dt_raw_2 = lambda k=s - 10: dt_raw(r + 1, k)
                        work = [lambda w=work: (w[0]() if w else None, dt_raw_2())] + work[1:]
                    slot(r, s, s % 2, work, before=scans)

            project_x(0)
            c_to_tok(0)
            for k in range(KC):
                dt_raw(0, k)
            round_(0, ffn=False)
            with pe.Fori(1, BATCH - 1) as r:
                round_(r)
            round_(BATCH - 1, setup=False)
            round_(BATCH, scans=False, setup=False)

        @block.scalar
        def _(act):
            def exps(r, s, par):
                wait(act, scan_done, 16 * r + s - 1)
                for j in range(KC):
                    nc.scalar.activation(dA[:, par, j, 1:SEQ], dt_chan[:, j, 1:SEQ], ACT.Exp,
                                         scale=A[:, j, ds(s, 1)]).then_inc(dA_ready, 1)

            def take_dt(r):
                act.wait_ge(dt_set, 4 * r + 4)
                wait(act, dA_ready, 64 * r)
                nc.scalar.copy(dt_chan[:], dt_next[:]).then_inc(dt_cur, 1)
                act.wait_ge(dt_cur, r + 1)

            def take_xp(b):
                if not is_first(b):
                    act.wait_ge(z_ps, 4 * b)
                    act.wait_ge(b_out, 16 * b)
                if not isinstance(b, int) or b > 2:
                    act.wait_ge(out_done, 64 * (b - 2))
                nc.scalar.activation(dtin, dtw_sb[:], ACT.Copy, bias=1.0, scale=0.0).then_inc(ones_set, 1)
                act.wait_ge(ones_set, b + 1)
                act.wait_ge(xp_ps, b + 1)
                nc.scalar.copy(dtin[0:RK, :], G[0][0:RK, :])
                nc.scalar.copy(xp, G[0][0:XR, :]).then_inc(xp_set, 1)

            def take_c(b):
                act.wait_ge(c_ps, b + 1)
                wait(act, C_set, b)
                nc.scalar.copy(C_next[:], G[1][:, 0:TC * 2 * NS].rearrange("p (c n) -> p c n", c=TC)[:, :, RK:RK + NS]
                               ).then_inc(cn_set, 1)

            def softplus_exp(b, k, r=0):
                n = 4 * b + k + 1
                act.wait_ge(z_ps, n)
                wait(act, dt_set, n - 2)
                if k == 0 and not is_first(r):
                    act.wait_ge(gate_ps, OT * r)
                    act.wait_ge(up_ps, OT * r)
                nc.scalar.activation(e_sp[k % 2], G[k % 2][:], ACT.Abs).then_inc(z_abs, 1)
                act.wait_ge(z_abs, n)
                nc.scalar.activation(e_sp[k % 2], e_sp[k % 2], ACT.Exp, scale=-1.0).then_inc(e_set, 1)

            def softplus_ln(b, k):
                act.wait_ge(r_set, 4 * b + k + 1)
                nc.scalar.activation(e_sp[k % 2], e_sp[k % 2], ACT.Ln, bias=1.0).then_inc(ln_set, 1)

            def high_x(r):
                for k in range(KC):
                    act.wait_ge(x2T_ps, 4 * (r - 1) + k + 1)
                    nc.scalar.activation(xh[:, k, :], F[:, k, :], ACT.Copy, scale=X_UP).then_inc(xh_set, 1)

            def silus(r, t):
                for q in range(2):
                    act.wait_ge(gate_ps, OT * (r - 1) + t + (q + 1))
                    act.wait_ge(h_set, OT * (r - 1) + t + (q + 1))
                    nc.scalar.activation(sh[:, q, :], F[:, q, :], ACT.Silu, scale=gs_sb[:, ds(t + q, 1)]).then_inc(silu_set, 1)

            def high_h(r, t):
                for q in range(2):
                    act.wait_ge(h_set, OT * (r - 1) + t + (q + 3))
                    nc.scalar.copy(hp[:, 0, ds(t + q, 1), :].rearrange("p a t -> p (a t)"), sh[:, 2 + q, :]).then_inc(hh_set, 1)

            def norm2(r, c):
                n = 4 * (r - 1) + c + 1
                act.wait_ge(ln2_nmr, n)
                nc.scalar.activation(ybuf[:, c, :], ybuf[:, c, :], ACT.Identity, bias=nmr2[:, c:c + 1],
                                     scale=rstd2[:, c:c + 1]).then_inc(out_set, 1)
                act.wait_ge(out_set, n)
                act.dma_start(out[ds((r - 1) * SEQ + c * P, P), :], ybuf[:, c, :]).then_inc(out_done, 16)

            def load_chan(r):
                act.wait_ge(u_set, r + 1)
                for k in range(KC):
                    act.dma_start(x_chan[:, k, :],
                                  xc_d[ds(r + 1, 1), k * P:(k + 1) * P, :].rearrange("a p t -> p (a t)")).then_inc(xc_in, 16)

            def load_tok(r):
                act.wait_ge(acc_done, 64 * r + 4)
                act.dma_start(x_tok[:], x_d[ds(r + 1, 1), :, :].rearrange("a (c p) d -> p (a c) d", p=P)).then_inc(x_in, 16)

            def convert(i):
                if 0 <= i < len(CH):
                    act.wait_ge(stage_in[i % NST], 16 * (i // NST + 1))
                    nc.scalar.copy(CH[i][1], place(i, CH[i][1])).then_inc(w_conv, 1)

            def late_slot(r, s, setup=True):
                if setup and s >= 11 and s <= 14:
                    softplus_ln(r + 1, s - 11)
                if setup and s <= 13:
                    softplus_exp(r + 1, s - 10, r)

            def round_(r, scans=True, ffn=True, setup=True, last3=True):
                if scans:
                    take_dt(r)
                    exps(r, 0, 0)
                    if setup:
                        load_chan(r)
                    exps(r, 1, 1)
                if last3:
                    norm2(r - 1, 3)
                if setup:
                    take_xp(r + 1)
                if ffn:
                    high_x(r)
                if scans:
                    exps(r, 2, 0)
                if setup:
                    take_c(r + 1)
                if ffn and scans:
                    act.wait_ge(u_set, r + 1)
                    apart(act)
                with act.Fori(0, 2) as i:
                    for n in range(4):
                        if ffn and n < 3:
                            silus(r, 6 * i + 2 * n)
                        if scans:
                            exps(r, 4 * i + (3 + n), (1 + n) % 2)
                        if ffn and n < 3:
                            high_h(r, 6 * i + 2 * n)
                if ffn:
                    silus(r, 12)
                    high_h(r, 12)
                if setup:
                    load_tok(r)
                late_slot(r, 10, setup)
                for s in range(11, NS):
                    if scans:
                        exps(r, s, s % 2)
                    late_slot(r, s, setup)
                    if ffn and s in DONE_BY:
                        norm2(r, DONE_BY.index(s))

            def round_0():
                take_dt(0)
                for s in range(NS):
                    exps(0, s, s % 2)
                    convert(s - 1)
                    if s == 2:
                        load_chan(0)
                        load_tok(0)
                    if s == 10:
                        take_xp(1)
                        take_c(1)
                    if s >= 10:
                        late_slot(0, s)

            act.wait_ge(const_in, 64)
            take_xp(0)
            take_c(0)
            for k in range(KC):
                softplus_exp(0, k)
                softplus_ln(0, k)
            act.wait_ge(al_in, 16)
            nc.scalar.activation(A[:], A[:], ACT.Exp).then_inc(A_exp, 1)
            act.wait_ge(A_set, 1)
            act.wait_ge(zero_set, 1)
            round_0()
            act.wait_ge(scales_set, 1)
            round_(1, last3=False)
            with act.Fori(2, BATCH - 1) as r:
                round_(r)
            round_(BATCH - 1, setup=False)
            round_(BATCH, scans=False, setup=False)
            norm2(BATCH, 3)
            act.wait_ge(out_done, 64 * BATCH)

        @block.gpsimd
        def _(pool):
            def b_slot(r, s, par, lane, fourth):
                pool.wait_ge(b_in[lane], 64 * r + 16 * fourth + 16)
                wait(pool, scan_done, 16 * r + s - 1)
                nc.gpsimd.tensor_tensor(dBx[:, par, :, :], u_chan[:],
                                        Bb[:, lane:lane + 1, :].to_broadcast([P, KC, SEQ]), ALU.mult).then_inc(dBx_ready, 1)

            def static_slot(r, s):
                b_slot(r, s, s % 2, s % 4, s // 4)

            def take_row(r):
                pool.wait_ge(dt_set, 4 * r + 4)
                wait(pool, dBx_ready, 16 * r)
                nc.gpsimd.tensor_tensor(u_chan[:], dt_next[:], x_chan[:], ALU.mult).then_inc(u_set, 1)
                pool.wait_ge(u_set, r + 1)

            def rstd1(r):
                pool.wait_ge(ln1_ve, r)
                nc.gpsimd.tensor_tensor(rstd[:], mv[:, :, 1], neg_half[:], ALU.pow).then_inc(ln1_rstd, 1)

            def rstd_2(r, c):
                pool.wait_ge(ln2_ve, 4 * (r - 1) + c + 1)
                nc.gpsimd.tensor_tensor(rstd2[:, c:c + 1], ve2[:, c:c + 1], neg_half[:, 0:1], ALU.pow).then_inc(ln2_rstd, 1)
                pool.wait_ge(ln2_rstd, 4 * (r - 1) + c + 1)
                nc.gpsimd.tensor_tensor(nmr2[:, c:c + 1], nm2[:, c:c + 1], rstd2[:, c:c + 1], ALU.mult).then_inc(ln2_nmr, 1)

            def low_h(r, t):
                for q in range(2):
                    pool.wait_ge(hh_set, OT * (r - 1) + t + (q + 1))
                    nc.gpsimd.tensor_tensor(hp[:, 1, ds(t + q, 1), :].rearrange("p a t -> p (a t)"), sh[:, 2 + q, :],
                                            hp[:, 0, ds(t + q, 1), :].rearrange("p a t -> p (a t)"),
                                            ALU.subtract).then_inc(hl_set, 1)

            def scale_x(r):
                pool.wait_ge(x_in, 16 * r + 16)
                nc.gpsimd.tensor_tensor(x_tok[:], x_tok[:], D1[:].rearrange("p (a d) -> p a d", a=1).to_broadcast([P, TC, D]),
                                        ALU.mult).then_inc(xd_set, 1)

            def round_(r, scans=True, ffn=True, last3=True, setup=True):
                if scans:
                    take_row(r)
                    static_slot(r, 0)
                    static_slot(r, 1)
                if last3:
                    rstd_2(r - 1, 3)
                if ffn:
                    rstd1(r)
                if scans:
                    static_slot(r, 2)
                with pool.Fori(0, 2) as i:
                    for n in range(4):
                        if scans:
                            b_slot(r, 4 * i + (3 + n), (1 + n) % 2, (3 + n) % 4, i + (3 + n) // 4)
                        if ffn and n < 3:
                            low_h(r, 6 * i + 2 * n)
                if ffn:
                    low_h(r, 12)
                for s in range(11, NS):
                    if scans:
                        static_slot(r, s)
                    if setup and s == 12:
                        scale_x(r + 1)
                    if ffn and s in DONE_BY:
                        rstd_2(r, DONE_BY.index(s))

            nc.gpsimd.memset(dA[:], 0.0).then_inc(zero_set, 1)
            nc.gpsimd.memset(neg_half[:], -0.5).then_inc(nh_set, 1)
            pool.sem_inc(hl_set, 2)
            pool.wait_ge(nh_set, 1)
            round_(0, ffn=False, last3=False)
            pool.wait_ge(c_par, 1)
            nc.gpsimd.partition_all_reduce(small[:, 1:2], small[:, 0:1], P, bass.bass_isa.ReduceOp.max).then_inc(c_all, 1)
            pool.wait_ge(c_all, 1)
            nc.gpsimd.tensor_tensor(small[:, 2:3], small[:, 1:2], neg_half[:, 0:1], ALU.pow).then_inc(c_pow, 1)
            round_(1, last3=False)
            with pool.Fori(2, BATCH - 1) as r:
                round_(r)
            round_(BATCH - 1, setup=False)
            round_(BATCH, scans=False, setup=False)
            rstd_2(BATCH, 3)

        @block.vector
        def _(dve):
            def scan(r, s, par):
                dve.wait_ge(dBx_ready, 16 * r + s + 1)
                dve.wait_ge(dA_ready, 64 * r + 4 * s + 4)
                wait(dve, H_done, 64 * r + 4 * s - 4)
                nc.vector.tensor_tensor_scan(h[:, par, :, :].rearrange("p k t -> p (k t)"),
                                             dA[:, par, :, :].rearrange("p k t -> p (k t)"),
                                             dBx[:, par, :, :].rearrange("p k t -> p (k t)"), 0.0,
                                             ALU.mult, ALU.add).then_inc(scan_done, 1)

            def add(r, s, c, n):
                dve.wait_ge(H_done, 64 * r + 4 * s - 3 + c)
                wait(dve, acc_done, 64 * r + 4 * s - 7 + c)
                before = x_tok if isinstance(n, int) and n == 0 else acc
                nc.vector.scalar_tensor_tensor(acc[:, c, :], H[c % 2][:], C_cur[:, c, ds(n, 1)], before[:, c, :],
                                               ALU.mult, ALU.add).then_inc(acc_done, 1)

            def slot(r, s, par, scans=True, between=()):
                if scans:
                    scan(r, s, par)
                for c in range(TC):
                    if c < len(between) and between[c] is not None:
                        between[c]()
                    if scans:
                        add(r, s, c, s - 1)
                if len(between) > TC:
                    between[TC]()

            def ln1_stats(r, c):
                dve.wait_ge(acc_done, 64 * r - 3 + c)
                apart(dve)
                nc.vector.bn_stats(st[:, c, :], acc[:, c, :]).then_inc(ln1_st, 1)

            def ln1_var(r):
                dve.wait_ge(ln1_st, 4 * r)
                apart(dve)
                for c in range(TC):
                    last = nc.vector.bn_aggr(mv[:, c, :], st[:, c, :])
                last.then_inc(ln1_mv, 1)
                dve.wait_ge(ln1_mv, r)
                nc.vector.tensor_scalar(mv[:, :, 1], mv[:, :, 1], EPS, None, ALU.add).then_inc(ln1_ve, 1)

            def ln1(r):
                dve.wait_ge(ln1_rstd, r)
                if not isinstance(r, int) or r > 1:
                    dve.wait_ge(y_set, 4 * r - 4)
                for c in range(TC):
                    nc.vector.tensor_scalar(x2[:, c, :], acc[:, c, :], mv[:, c, 0:1], rstd[:, c:c + 1],
                                            ALU.subtract, ALU.mult).then_inc(x2_set, 1)

            def take_C(r):
                dve.wait_ge(cn_set, r + 1)
                nc.vector.tensor_copy(C_cur[:], C_next[:]).then_inc(C_set, 1)
                dve.wait_ge(C_set, r + 1)
                dve.wait_ge(xd_set, r + 1)

            def softplus_lost(b, k):
                n = 4 * b + k + 1
                dve.wait_ge(e_set, n)
                nc.vector.tensor_scalar(t_sp[k % 2], e_sp[k % 2], 1.0, -1.0, ALU.add, ALU.add).then_inc(w1_set, 1)
                dve.wait_ge(w1_set, n)
                nc.vector.tensor_tensor(t_sp[k % 2], e_sp[k % 2], t_sp[k % 2], ALU.subtract).then_inc(r_set, 1)

            def softplus_sum(b, k):
                n = 4 * b + k + 1
                dve.wait_ge(ln_set, n)
                nc.vector.tensor_tensor(t_sp[k % 2], t_sp[k % 2], e_sp[k % 2], ALU.add).then_inc(l_set, 1)
                dve.wait_ge(l_set, n)
                nc.vector.scalar_tensor_tensor(dt_next[:, k, :], G[k % 2][:], 0.0, t_sp[k % 2], ALU.max, ALU.add
                                               ).then_inc(dt_set, 1)

            def low_x(r):
                for k in range(KC):
                    dve.wait_ge(xh_set, 4 * (r - 1) + k + 1)
                    nc.vector.scalar_tensor_tensor(xl[:, k, :], F[:, k, :], X_UP, xh[:, k, :],
                                                   ALU.mult, ALU.subtract).then_inc(xl_set, 1)

            def tiles(r, t, qs=range(2)):
                for q in qs:
                    dve.wait_ge(up_ps, OT * (r - 1) + t + (q + 1))
                    dve.wait_ge(silu_set, OT * (r - 1) + t + (q + 1))
                    dve.wait_ge(hl_set, OT * (r - 1) + t + (q + 1))
                    nc.vector.scalar_tensor_tensor(sh[:, 2 + q, :], F[:, 2 + q, :], us_sb[:, ds(t + q, 1)], sh[:, q, :],
                                                   ALU.mult, ALU.mult).then_inc(h_set, 1)

            def finish(r, c, setup):
                n = 4 * (r - 1) + c + 1
                dve.wait_ge(down_ps, n)
                if not isinstance(r, int):
                    dve.wait_ge(out_done, 64 * r - 64)
                elif r > 1:
                    dve.wait_ge(out_done, 64 * (r - 1))
                if setup and c == 2:
                    dve.wait_ge(b_out, 16 * r + 32)
                    dve.wait_ge(cn_set, r + 2)
                if setup and c == 3:
                    dve.wait_ge(z_ps, 4 * r + 8)
                nc.vector.tensor_tensor(ybuf[:, c, :], F[:, c, :], ds_bc[:], ALU.mult).then_inc(ds_done, 1)
                dve.wait_ge(ds_done, n)
                nc.vector.tensor_tensor(ybuf[:, c, :], ybuf[:, c, :], x2[:, c, :], ALU.add).then_inc(y_set, 1)
                dve.wait_ge(y_set, n)
                apart(dve)
                nc.vector.bn_stats(st2[:], ybuf[:, c, :]).then_inc(ln2_st, 1)
                dve.wait_ge(ln2_st, n)
                apart(dve)
                nc.vector.bn_aggr(mv2[:], st2[:]).then_inc(ln2_mv, 1)
                dve.wait_ge(ln2_mv, n)
                nc.vector.tensor_scalar(nm2[:, c:c + 1], mv2[:, 0:1], -1.0, None, ALU.mult)
                nc.vector.tensor_scalar(ve2[:, c:c + 1], mv2[:, 1:2], EPS, None, ALU.add).then_inc(ln2_ve, 1)
                dve.wait_ge(ln2_ve, n)

            def round_(r, scans=True, ffn=True, setup=True):
                if scans:
                    scan(r, 0, 0)
                if ffn:
                    for c in range(TC):
                        add(r, 0, c, NS - 1)
                        if c > 0:
                            ln1_stats(r, c - 1)
                    ln1_stats(r, TC - 1)
                    ln1_var(r)
                if ffn:
                    ln1(r)
                    dve.wait_ge(x2_set, 4 * r)
                if scans:
                    take_C(r)
                    add(r, 1, 0, 0)
                    add(r, 1, 1, 0)
                if ffn:
                    low_x(r)
                if scans:
                    scan(r, 1, 1)
                    add(r, 1, 2, 0)
                    add(r, 1, 3, 0)
                if ffn:
                    if scans:
                        dve.wait_ge(u_set, r + 1)
                        dve.wait_ge(dt_cur, r + 1)
                        apart(dve)
                with dve.Fori(0, 2) as i:
                    for n in range(4):
                        halves = [lambda q=q, n=n: tiles(r, 6 * i + 2 * n, qs=(q,)) for q in range(2)] if ffn and n < 3 else []
                        slot(r, 4 * i + (2 + n), n % 2, scans, [None] * min(n, 2) + halves)
                for s in range(10, NS):
                    between = [None] * 5
                    if ffn and s == 10:
                        between = [lambda: tiles(r, 12, qs=(0,)), lambda: tiles(r, 12, qs=(1,)), None, None, None]
                    if setup and s <= 13:
                        between[3] = lambda k=s - 10: softplus_lost(r + 1, k)
                    if setup and 11 <= s <= 14:
                        between[1] = lambda k=s - 11: softplus_sum(r + 1, k)
                    if ffn and s in DOWN_BY:
                        between[4] = lambda c=DOWN_BY.index(s): finish(r, c, setup)
                    between = between if between[4] else between[:4]
                    slot(r, s, s % 2, scans, between)

            dve.sem_inc(h_set, 2)
            for k in range(KC):
                softplus_lost(0, k)
                softplus_sum(0, k)
            dve.wait_ge(A_exp, 1)
            nc.vector.tensor_scalar(A[:], A[:], -1.0, None, ALU.mult).then_inc(A_set, 1)
            dve.wait_ge(scale_in, 64)
            nc.vector.tensor_scalar(D1[:], D1[:], 1.0, None, ALU.add).then_inc(D1_set, 1)
            dve.wait_ge(D1_set, 1)
            dve.wait_ge(x_in, 16)
            nc.vector.tensor_tensor(x_tok[:], x_tok[:], D1[:].rearrange("p (a d) -> p a d", a=1).to_broadcast([P, TC, D]),
                                    ALU.mult).then_inc(xd_set, 1)
            nc.vector.tensor_tensor(gu[:], gs_sb[:], us_sb[:], ALU.mult).then_inc(c_gu, 1)
            dve.wait_ge(c_gu, 1)
            nc.vector.tensor_tensor(gu[:], gu[:], gu[:], ALU.mult).then_inc(c_sq, 1)
            dve.wait_ge(c_sq, 1)
            nc.vector.reduce_max(small[:, 0:1], gu[:], AXX).then_inc(c_max, 1)
            dve.wait_ge(c_max, 1)
            nc.vector.tensor_scalar(small[:, 0:1], small[:, 0:1], 1e-30, None, ALU.max).then_inc(c_par, 1)
            round_(0, ffn=False)
            dve.wait_ge(c_pow, 1)
            nc.vector.tensor_scalar(small[:, 3:4], small[:, 2:3], H_TOP / H_BOUND, None, ALU.mult).then_inc(c_set, 1)
            dve.wait_ge(c_set, 1)
            nc.vector.reciprocal(small[:, 4:5], small[:, 3:4]).then_inc(c_inv, 1)
            dve.wait_ge(c_inv, 1)
            nc.vector.tensor_scalar(ds_bc[:], ds_bc[:], small[:, 4:5], None, ALU.mult)
            nc.vector.tensor_scalar(us_sb[:], us_sb[:], small[:, 3:4], 1.0 / X_UP, ALU.mult, ALU.mult)
            nc.vector.tensor_scalar(gs_sb[:], gs_sb[:], 1.0 / X_UP, None, ALU.mult).then_inc(scales_set, 1)
            dve.wait_ge(scales_set, 1)
            with dve.Fori(1, BATCH - 1) as r:
                round_(r)
            round_(BATCH - 1, setup=False)
            round_(BATCH, scans=False, setup=False)


def kernel(**inputs):
    import numpy as np
    import concourse.bacc as bacc
    from concourse.bass_utils import run_bass_kernel_spmd

    a = {k.replace("L0_attn_", "").replace("L0_ffn_", ""): np.asarray(val) for k, val in inputs.items()}

    def t_(w):
        return np.ascontiguousarray(w.T)

    arrays = {
        "x": np.ascontiguousarray(a["x"]),
        "x_chan": np.ascontiguousarray(a["x"].transpose(0, 2, 1)),
        "A_log": np.ascontiguousarray(a["A_log"]),
        "Dw": a["D"].reshape(1, -1),
        "xproj": t_(np.concatenate([a["x_proj_w"][:RK], a["x_proj_w"][RK + NS:], a["x_proj_w"][RK:RK + NS]])),
        "dtw": t_(a["dt_proj_w"]),
        "dt_b": a["dt_proj_b"].reshape(1, -1),
        "wg": t_(a["gate_wq"]),
        "gs": t_(a["gate_scale"].reshape(-1, 128)),
        "wu": t_(a["up_wq"]),
        "us": t_(a["up_scale"].reshape(-1, 128)),
        "wd": t_(a["down_wq"]),
        "dscale": a["down_scale"].reshape(1, -1),
        "identity": np.eye(128, dtype=np.float32),
    }
    nc = bacc.Bacc("TRN2", target_bir_lowering=False, num_devices=1)
    args = [nc.dram_tensor(f"in_{n}", v.shape, mybir.dt.from_np(v.dtype), kind="ExternalInput").ap()
            for n, v in arrays.items()]
    out = nc.dram_tensor("out_y", (BATCH * SEQ, D), fp32, kind="ExternalOutput").ap()
    build(nc, *args, out)
    r = run_bass_kernel_spmd(nc, [{f"in_{n}": v for n, v in arrays.items()}], core_ids=[0])
    return r.results[0]["out_y"].reshape(BATCH, SEQ, D)
```

```python
import concourse.bass as bass
from concourse import mybir
from contextlib import ExitStack

P = 128
BATCH, SEQ, D = 4, 512, 512
TC, KC = SEQ // P, D // P
NS, RK = 16, 16
XR = RK + 2 * NS
INTER = 1792
OT = INTER // P
SLOTS = NS
EPS = 1e-5
X_UP = 2048.0
W_MAX = 128.0
H_BOUND = (1.02 * D * W_MAX) ** 2
H_TOP = 60000.0

fp32, fp16, i32 = mybir.dt.float32, mybir.dt.float16, mybir.dt.int32
ALU = mybir.AluOpType
ACT = mybir.ActivationFunctionType
ds = bass.ds


def build(nc, x_d, xc_d, A_log, Dw, xproj, dtw, dt_b, wg, gs, wu, us, wd, dscale, identity, out):
    ctx = ExitStack()
    with ctx:
        def sb(name, shape, dt=fp32):
            return ctx.enter_context(nc.sbuf_tensor(name, shape, dt))

        def sem(name):
            return ctx.enter_context(nc.semaphore(name))

        ident = sb("ident", [P, P])
        A = sb("A", [P, KC, NS])
        D1 = sb("D1", [P, D])
        ds_bc = sb("ds_bc", [P, D])
        xw = sb("xw", [P, KC, XR])
        dtw_sb = sb("dtw_sb", [RK + 1, D])
        gs_sb = sb("gs_sb", [P, OT])
        us_sb = sb("us_sb", [P, OT])
        small = sb("small", [P, 5])
        gu = sb("gu", [P, OT])
        neg_half = sb("neg_half", [P, TC])
        wg16 = sb("wg16", [P, KC, INTER], fp16)
        wu16 = sb("wu16", [P, KC, INTER], fp16)
        wd16 = sb("wd16", [P, OT, D], fp16)
        x_tok = sb("x_tok", [P, TC, D])
        x_chan = sb("x_chan", [P, KC, SEQ])
        dt_chan = sb("dt_chan", [P, KC, SEQ])
        u_chan = sb("u_chan", [P, KC, SEQ])
        C_next = sb("C_next", [P, TC, NS])
        C_cur = sb("C_cur", [P, TC, NS])
        acc = sb("acc", [P, TC, D])
        x2 = sb("x2", [P, TC, D])
        ybuf = sb("ybuf", [P, TC, D])
        st = sb("st", [P, TC, 6])
        mv = sb("mv", [P, TC, 2])
        rstd = sb("rstd", [P, TC])
        st2 = sb("st2", [P, TC, 6])
        mv2 = sb("mv2", [P, TC, 2])
        ve2 = sb("ve2", [P, TC])
        nm2 = sb("nm2", [P, TC])
        rstd2 = sb("rstd2", [P, TC])
        nmr2 = sb("nmr2", [P, TC])
        Bb = sb("Bb", [P, 4, SEQ])
        dBx = sb("dBx", [P, 2, KC, SEQ])
        dA = sb("dA", [P, 2, KC, SEQ])
        h = sb("h", [P, 2, KC, SEQ])
        xh = sb("xh", [P, KC, SEQ], fp16)
        xl = sb("xl", [P, KC, SEQ], fp16)
        sh = sb("sh", [P, 4, SEQ])
        hp = sb("hp", [P, 2, OT, SEQ], fp16)
        stage = hp[:].rearrange("p a b c -> p (a b c)").bitcast(i32)
        dt_next = sh
        xh32 = xh[:].rearrange("p a b -> p (a b)").bitcast(fp32).rearrange("p (a b) -> p a b", a=2)
        xl32 = xl[:].rearrange("p a b -> p (a b)").bitcast(fp32).rearrange("p (a b) -> p a b", a=2)
        e_sp, t_sp = [xh32[:, 0, :], xl32[:, 0, :]], [xh32[:, 1, :], xl32[:, 1, :]]
        e_first, t_first, l_first = h[:, 0], h[:, 1], sh
        dtin = ybuf[0:RK + 1, 3, :]
        xp = ybuf[0:XR, 2, :]

        H = [ctx.enter_context(nc.psum_tensor(f"psH{i}", [P, D], fp32)) for i in range(2)]
        F = ctx.enter_context(nc.psum_tensor("psF", [P, 4, 512], fp32))
        G = [ctx.enter_context(nc.psum_tensor(f"psG{i}", [P, 512], fp32)) for i in range(2)]
        B_dram = nc.dram_tensor("B_rows", (2, NS, SEQ), fp32, kind="Internal").ap()

        def sems(*names):
            return [sem(n) for n in names]

        const_in, scale_in, x_in, xc_in, al_in, out_done, b_out = sems(
            "const_in", "scale_in", "x_in", "xc_in", "al_in", "out_done", "b_out")
        x_first_in = sems("x_first_in0", "x_first_in1", "x_first_in2", "x_first_in3")
        xw_in, dtin_set, u_half, dBx_half = sems("xw_in", "dtin_set", "u_half", "dBx_half")
        b_in = sems("b_in0", "b_in1", "b_in2", "b_in3")
        A_exp, A_set, D1_set, nh_set, zero_set = sems("A_exp", "A_set", "D1_set", "nh_set", "zero_set")
        c_gu, c_sq, c_max, c_par, c_all, c_pow, c_set, c_inv, scales_set = sems(
            "c_gu", "c_sq", "c_max", "c_par", "c_all", "c_pow", "c_set", "c_inv", "scales_set")
        went_on = sem("went_on")
        w_conv = sem("w_conv")
        dBx_ready, scan_done = sems("dBx_ready", "scan_done")
        dA_ready, H_done, acc_done = sems("dA_ready", "H_done", "acc_done")
        xp_ps, ones_set, xp_set, c_ps, cn_set, dt_cur, u_set, C_set, xd_set = sems(
            "xp_ps", "ones_set", "xp_set", "c_ps", "cn_set", "dt_cur", "u_set", "C_set", "xd_set")
        z_ps, z_abs, e_set, w_set, w1_set, r_set, ln_set, l_set, dt_set = sems(
            "z_ps", "z_abs", "e_set", "w_set", "w1_set", "r_set", "ln_set", "l_set", "dt_set")
        ln1_st, ln1_mv, ln1_ve, ln1_rstd, x2_set, x2T_ps, xh_set, xl_set = sems(
            "ln1_st", "ln1_mv", "ln1_ve", "ln1_rstd", "x2_set", "x2T_ps", "xh_set", "xl_set")
        gate_ps, up_ps, silu_set, h_set, hh_set, hl_set = sems(
            "gate_ps", "up_ps", "silu_set", "h_set", "hh_set", "hl_set")
        down_ps, ds_done, y_set, ln2_st, ln2_mv, ln2_ve, ln2_rstd, ln2_nmr, out_set = sems(
            "down_ps", "ds_done", "y_set", "ln2_st", "ln2_mv", "ln2_ve", "ln2_rstd", "ln2_nmr", "out_set")

        block = ctx.enter_context(nc.Block())

        def wait(eng, s, value):
            if not isinstance(value, int) or value > 0:
                eng.wait_ge(s, value)

        def apart(eng):
            eng.sem_inc(went_on, 1)

        def w_chunks():
            for k in range(KC):
                yield wg[k * P:(k + 1) * P, :], wg16[:, k, :]
                yield wu[k * P:(k + 1) * P, :], wu16[:, k, :]
            for t0 in range(0, OT, 3):
                n = min(3, OT - t0)
                yield (wd.rearrange("(t p) d -> p t d", p=P)[:, t0:t0 + n, :],
                       wd16[:, t0:t0 + n, :])
        CHUNKS = list(w_chunks())
        PLACES = OT * SEQ // INTER
        stage_in = [sem(f"stage_in{i}") for i in range(PLACES)]

        def place(i, dst):
            if len(dst.shape) == 2:
                return stage[:, (i % PLACES) * INTER:(i % PLACES) * INTER + INTER]
            n = dst.shape[1]
            return stage[:, (i % PLACES) * INTER:(i % PLACES) * INTER + n * D].rearrange("p (t d) -> p t d", d=D)

        DOWN_BY = (12, 13, 14, 15)
        DONE_BY = (14, 15)
        SUM_AT = ((11, 4), (12, 0), (13, 4), (14, 0))

        def is_first(r):
            return isinstance(r, int) and r == 0

        def bank(r, c):
            return F[:, c, :] if is_first(r) and c >= 2 else H[c % 2][:]

        @block.sync
        def _(sp):
            for k in range(KC):
                sp.dma_start(x_chan[:, k, :], xc_d[0, k * P:(k + 1) * P, :]).then_inc(x_first_in[k], 16)
                if k == 0:
                    sp.dma_start(xw[:], xproj.rearrange("(k p) r -> p k r", p=P)).then_inc(xw_in, 16)
            sp.dma_start(dtw_sb[0:RK, :], dtw).then_inc(const_in, 16)
            sp.dma_start(dtw_sb[RK:RK + 1, :], dt_b).then_inc(const_in, 16)
            sp.dma_start(ident[:], identity).then_inc(const_in, 16)
            sp.dma_start(A[:], A_log.rearrange("(k p) n -> p k n", p=P)).then_inc(al_in, 16)
            sp.dma_start(x_tok[:], x_d[0].rearrange("(c p) d -> p c d", p=P)).then_inc(x_in, 16)
            sp.dma_start(D1[:], Dw.to_broadcast([P, D])).then_inc(scale_in, 16)
            sp.dma_start(ds_bc[:], dscale.to_broadcast([P, D])).then_inc(scale_in, 16)
            sp.dma_start(gs_sb[:], gs).then_inc(scale_in, 16)
            sp.dma_start(us_sb[:], us).then_inc(scale_in, 16)

            def load_weights(i):
                if i < len(CHUNKS):
                    wait(sp, w_conv, i - PLACES + 1)
                    sp.dma_start(place(i, CHUNKS[i][1]), CHUNKS[i][0]).then_inc(stage_in[i % PLACES], 16)

            def rows_out(b, parity):
                sp.wait_ge(xp_set, b + 1)
                sp.dma_start(B_dram[parity], xp[RK + NS:XR, :]).then_inc(b_out, 16)

            def b_slot(r, s, parity, lane):
                wait(sp, dBx_ready, 16 * r + s - 3)
                sp.dma_start(Bb[:, lane, :], B_dram[parity, ds(s, 1), :].to_broadcast([P, SEQ])).then_inc(b_in[lane], 16)

            def four_slots(r, parity, first, weights=None):
                for n in range(4):
                    b_slot(r, first + n, parity, n)
                    if weights is not None:
                        load_weights(weights + n)

            rows_out(0, 0)
            sp.wait_ge(b_out, 16)
            for s in range(0, NS, 4):
                four_slots(0, 0, s, weights=s)
                if s == 8:
                    rows_out(1, 1)
            for r in range(1, BATCH):
                sp.wait_ge(b_out, 16 * (r + 1))
                with sp.Fori(0, 3) as i:
                    four_slots(r, r % 2, i * 4)
                if r + 1 < BATCH:
                    rows_out(r + 1, (r + 1) % 2)
                four_slots(r, r % 2, 12)
            sp.wait_ge(b_out, 16 * BATCH)

        @block.tensor
        def _(pe):
            def h_to_tok(r, s, par, c):
                if c == 0:
                    pe.wait_ge(scan_done, 16 * r + s)
                wait(pe, acc_done, 64 * r + 4 * s - (7 if is_first(r) else 5) + c)
                for k in range(KC):
                    last = nc.tensor.transpose(bank(r, c)[:, k * P:(k + 1) * P], h[:, 1 - par, k, c * P:(c + 1) * P], ident[:])
                last.then_inc(H_done, 1)

            def slot(r, s, par, work=(), before=True):
                for j in range(4):
                    if before:
                        h_to_tok(r, s, par, j)
                    if j < len(work):
                        work[j]()

            def product(w16, bank, t, done, x2_of=None):
                for k in range(KC):
                    if x2_of is not None:
                        pe.wait_ge(xh_set, 4 * (x2_of - 1) + k + 1)
                        pe.wait_ge(xl_set, 4 * (x2_of - 1) + k + 1)
                    for i, part in enumerate((xh, xl)):
                        last = nc.tensor.matmul(F[:, bank, :], w16[:, k, ds(t * P, P)], part[:, k, :],
                                                start=(k == 0 and i == 0), stop=(k == KC - 1 and i == 1))
                last.then_inc(done, 1)

            def gate(r, t, q, first=False):
                if not first:
                    pe.wait_ge(silu_set, OT * (r - 1) + t - 1)
                product(wg16, q, t, gate_ps, r if first and t == 0 else None)

            def up(r, t, q, first=False):
                if not first:
                    pe.wait_ge(h_set, OT * (r - 1) + t + 1)
                product(wu16, 2 + q, t, up_ps)

            def tiles(r, t):
                return [lambda: gate(r, t, 0), lambda: gate(r, t + 1, 1), lambda: up(r, t, 0), lambda: up(r, t + 1, 1)]

            def project_x(b):
                if is_first(b):
                    pe.wait_ge(xw_in, 16)
                else:
                    pe.wait_ge(xc_in, 64 * b)
                    pe.wait_ge(dt_set, 4 * b)
                for k in range(KC):
                    if is_first(b):
                        pe.wait_ge(x_first_in[k], 16)
                    last = nc.tensor.matmul(G[0][0:XR, :], xw[:, k, :], x_chan[:, k, :], start=(k == 0), stop=(k == KC - 1))
                last.then_inc(xp_ps, 1)

            def c_to_tok(b):
                pe.wait_ge(xp_set, b + 1)
                apart(pe)
                for c in range(TC):
                    last = nc.tensor.transpose(G[1][:, c * 2 * NS:(c + 1) * 2 * NS], xp[0:2 * NS, c * P:(c + 1) * P],
                                               ident[0:2 * NS, 0:2 * NS])
                last.then_inc(c_ps, 1)

            def dt_raw(b, k):
                if k == 1:
                    pe.wait_ge(cn_set, b + 1)
                if k > 1:
                    pe.wait_ge(dt_set, 4 * b + k - 1)
                nc.tensor.matmul(G[k % 2][:], dtw_sb[:, k * P:(k + 1) * P], dtin, start=True, stop=True).then_inc(z_ps, 1)

            def x2_to_chan(r):
                for c in range(TC):
                    pe.wait_ge(x2_set, 4 * r - 3 + c)
                    for k in range(KC):
                        done = nc.tensor.transpose(F[:, k, c * P:(c + 1) * P], x2[:, c, k * P:(k + 1) * P], ident[:])
                        if c == TC - 1:
                            done.then_inc(x2T_ps, 1)

            DOWN = [(c, part, t) for part in (0, 1) for c in (0, 1) for t in range(OT)]
            DOWN += [(c, part, t) for c in (2, 3) for part in (0, 1) for t in range(OT)]

            DT_AT = (0, 1)

            SHARE = 5

            def down(r, first, after):
                for n, (c, part, t) in list(enumerate(DOWN))[first:after]:
                    if n == 0:
                        pe.wait_ge(silu_set, OT * r)
                        pe.wait_ge(hh_set, OT * r - 2)
                    if n == OT - 2:
                        pe.wait_ge(hh_set, OT * r)
                    if n == 2 * OT:
                        pe.wait_ge(hl_set, OT * r)
                    if n == 2 * OT + OT - 2:
                        pe.wait_ge(hl_set, OT * r + 2)
                    if n == 4 * OT:
                        pe.wait_ge(h_set, OT * r + 2)
                    last = nc.tensor.matmul(F[:, c, :], hp[:, part, t, c * P:(c + 1) * P], wd16[:, t, :],
                                            start=(part == 0 and t == 0), stop=(part == 1 and t == OT - 1))
                    if part == 1 and t == OT - 1:
                        last.then_inc(down_ps, 1)

            def round_(r, scans=True, ffn=True, setup=True):
                slot(r, 0, 0, before=ffn)
                if ffn:
                    if setup:
                        project_x(r + 1)
                    if scans:
                        h_to_tok(r, 1, 1, 0)
                        h_to_tok(r, 1, 1, 1)
                    x2_to_chan(r)
                    if setup:
                        c_to_tok(r + 1)
                        dt_raw(r + 1, 0)
                    pe.wait_ge(w_conv, len(CHUNKS))
                    gate(r, 0, 0, first=True)
                    if scans:
                        h_to_tok(r, 1, 1, 2)
                    gate(r, 1, 1, first=True)
                    if scans:
                        h_to_tok(r, 1, 1, 3)
                    up(r, 0, 0, first=True)
                    up(r, 1, 1, first=True)
                    if setup:
                        dt_raw(r + 1, 1)
                else:
                    slot(r, 1, 1)
                    project_x(r + 1)
                with pe.Fori(0, 2) as i:
                    work = tiles(r, 6 * i + 2) + tiles(r, 6 * i + 4) + tiles(r, 6 * i + 6) if ffn else []
                    for n in range(4):
                        slot(r, 4 * i + (2 + n), n % 2, work[3 * n:3 * n + 3], before=scans)
                for s in range(10, NS):
                    work = [lambda q=q: down(r, SHARE * q, SHARE * (q + 1))
                            for q in range(4 * (s - 10), 4 * (s - 9))] if ffn else []
                    if setup and not ffn and s == 10:
                        work = [lambda: c_to_tok(r + 1), lambda: dt_raw(r + 1, 0), lambda: dt_raw(r + 1, 1)]
                    if setup and s == 12:
                        work = [lambda j=j, w=work: (w[j]() if w else None,
                                                     [dt_raw(r + 1, k) for k in (2, 3) if j == DT_AT[k - 2]])
                                for j in range(4)]
                    slot(r, s, s % 2, work, before=scans)

            project_x(0)
            pe.wait_ge(const_in, 48)
            pe.wait_ge(dtin_set, 1)
            for k in range(KC):
                nc.tensor.matmul(F[:, k, :], dtw_sb[:, k * P:(k + 1) * P], dtin, start=True, stop=True).then_inc(z_ps, 1)
            c_to_tok(0)
            round_(0, ffn=False)
            with pe.Fori(1, BATCH - 1) as r:
                round_(r)
            round_(BATCH - 1, setup=False)
            round_(BATCH, scans=False, setup=False)

        @block.scalar
        def _(act):
            def exps(r, s, par):
                wait(act, scan_done, 16 * r + s - 1)
                for j in range(KC):
                    nc.scalar.activation(dA[:, par, j, 1:SEQ], dt_chan[:, j, 1:SEQ], ACT.Exp,
                                         scale=A[:, j, ds(s, 1)]).then_inc(dA_ready, 1)

            def take_dt(r):
                act.wait_ge(dt_set, 4 * r + 4)
                wait(act, dA_ready, 64 * r)
                nc.scalar.copy(dt_chan[:], dt_next[:]).then_inc(dt_cur, 1)
                act.wait_ge(dt_cur, r + 1)

            def take_xp(b):
                if not is_first(b):
                    act.wait_ge(z_ps, 4 * b)
                    act.wait_ge(b_out, 16 * b)
                if not isinstance(b, int) or b > 2:
                    act.wait_ge(out_done, 64 * (b - 2))
                nc.scalar.activation(dtin, dtw_sb[:], ACT.Copy, bias=1.0, scale=0.0).then_inc(ones_set, 1)
                act.wait_ge(ones_set, b + 1)
                act.wait_ge(xp_ps, b + 1)
                nc.scalar.copy(dtin[0:RK, :], G[0][0:RK, :]).then_inc(dtin_set, 1)
                nc.scalar.copy(xp, G[0][0:XR, :]).then_inc(xp_set, 1)

            def take_c(b):
                act.wait_ge(c_ps, b + 1)
                wait(act, C_set, b)
                nc.scalar.copy(C_next[:], G[1][:, 0:TC * 2 * NS].rearrange("p (c n) -> p c n", c=TC)[:, :, RK:RK + NS]
                               ).then_inc(cn_set, 1)

            def softplus_exp(b, k0, r=0):
                n = 4 * b + k0 + 1
                if k0 == 0 and not is_first(r):
                    act.wait_ge(gate_ps, OT * r)
                    act.wait_ge(up_ps, OT * r)
                for q in range(2):
                    act.wait_ge(z_ps, n + q)
                    wait(act, dt_set, n + q - 2)
                    nc.scalar.activation(e_sp[q], G[q][:], ACT.Abs).then_inc(z_abs, 1)
                for q in range(2):
                    act.wait_ge(z_abs, n + q)
                    nc.scalar.activation(e_sp[q], e_sp[q], ACT.Exp, scale=-1.0).then_inc(e_set, 1)
                for q in range(2):
                    act.wait_ge(e_set, n + q)
                    nc.scalar.activation(t_sp[q], e_sp[q], ACT.Copy, bias=1.0).then_inc(w_set, 1)
                for q in range(2):
                    act.wait_ge(w_set, n + q)
                    nc.scalar.activation(t_sp[q], t_sp[q], ACT.Copy, bias=-1.0).then_inc(w1_set, 1)

            def softplus_ln(b, k):
                act.wait_ge(r_set, 4 * b + k + 1)
                nc.scalar.activation(e_sp[k % 2], e_sp[k % 2], ACT.Ln, bias=1.0).then_inc(ln_set, 1)

            def high_x(r):
                for k in range(KC):
                    act.wait_ge(x2T_ps, 4 * (r - 1) + k + 1)
                    nc.scalar.activation(xh[:, k, :], F[:, k, :], ACT.Copy, scale=X_UP).then_inc(xh_set, 1)

            def silus(r, t):
                for q in range(2):
                    act.wait_ge(gate_ps, OT * (r - 1) + t + (q + 1))
                    act.wait_ge(h_set, OT * (r - 1) + t + (q + 1))
                    nc.scalar.activation(sh[:, q, :], F[:, q, :], ACT.Silu, scale=gs_sb[:, ds(t + q, 1)]).then_inc(silu_set, 1)

            def high_h(r, t):
                for q in range(2):
                    act.wait_ge(h_set, OT * (r - 1) + t + (q + 3))
                    nc.scalar.copy(hp[:, 0, ds(t + q, 1), :].rearrange("p a t -> p (a t)"), sh[:, 2 + q, :]).then_inc(hh_set, 1)

            def norm2(r, c):
                n = 4 * (r - 1) + c + 1
                act.wait_ge(ln2_nmr, n)
                nc.scalar.activation(ybuf[:, c, :], ybuf[:, c, :], ACT.Identity, bias=nmr2[:, c:c + 1],
                                     scale=rstd2[:, c:c + 1]).then_inc(out_set, 1)
                act.wait_ge(out_set, n)
                act.dma_start(out[ds((r - 1) * SEQ + c * P, P), :], ybuf[:, c, :]).then_inc(out_done, 16)

            def load_chan(r):
                act.wait_ge(u_set, r + 1)
                if is_first(r):
                    act.wait_ge(u_half, 1)
                for k in range(KC):
                    act.dma_start(x_chan[:, k, :],
                                  xc_d[ds(r + 1, 1), k * P:(k + 1) * P, :].rearrange("a p t -> p (a t)")).then_inc(xc_in, 16)

            def load_tok(r):
                act.wait_ge(acc_done, 64 * r + 4)
                act.dma_start(x_tok[:], x_d[ds(r + 1, 1), :, :].rearrange("a (c p) d -> p (a c) d", p=P)).then_inc(x_in, 16)

            def convert(i):
                if 0 <= i < len(CHUNKS):
                    act.wait_ge(stage_in[i % PLACES], 16 * (i // PLACES + 1))
                    nc.scalar.copy(CHUNKS[i][1], place(i, CHUNKS[i][1])).then_inc(w_conv, 1)

            def late_slot(r, s, setup=True):
                if setup and s in (11, 13):
                    softplus_exp(r + 1, s - 11, r)
                if setup and s in (12, 14):
                    softplus_ln(r + 1, s - 12)
                    softplus_ln(r + 1, s - 11)

            def round_(r, scans=True, ffn=True, setup=True, last2=True):
                if scans:
                    take_dt(r)
                    exps(r, 0, 0)
                    if setup:
                        load_chan(r)
                if last2:
                    norm2(r - 1, 2)
                if scans:
                    exps(r, 1, 1)
                if last2:
                    norm2(r - 1, 3)
                if setup:
                    take_xp(r + 1)
                if ffn:
                    high_x(r)
                if scans:
                    exps(r, 2, 0)
                if setup:
                    take_c(r + 1)
                if ffn and scans:
                    act.wait_ge(u_set, r + 1)
                    apart(act)
                if isinstance(r, int) and r == 1:
                    act.wait_ge(scales_set, 1)
                with act.Fori(0, 2) as i:
                    for n in range(4):
                        if ffn and n < 3:
                            silus(r, 6 * i + 2 * n)
                        if scans:
                            exps(r, 4 * i + (3 + n), (1 + n) % 2)
                        if ffn and n < 3:
                            high_h(r, 6 * i + 2 * n)
                if ffn:
                    silus(r, 12)
                if scans:
                    exps(r, 11, 1)
                if ffn:
                    high_h(r, 12)
                if setup:
                    load_tok(r)
                for s in range(11, NS):
                    if scans and s > 11:
                        exps(r, s, s % 2)
                    late_slot(r, s, setup)
                    if ffn and s in DONE_BY:
                        norm2(r, DONE_BY.index(s))

            def round_0():
                act.wait_ge(dt_set, KC)
                act.sem_inc(dt_cur, 1)
                for s in range(NS):
                    exps(0, s, s % 2)
                    if s != 11:
                        convert(s - 1 if s < 11 else s - 2)
                    if s == 0:
                        load_chan(0)
                    if s == 2:
                        take_xp(1)
                        load_tok(0)
                    if s == 11:
                        take_c(1)
                    if s >= 10:
                        late_slot(0, s)

            act.wait_ge(const_in, 48)
            take_xp(0)
            for j in range(0, KC, 2):
                for k in (j, j + 1):
                    act.wait_ge(z_ps, k + 1)
                    nc.scalar.activation(e_first[:, k, :], F[:, k, :], ACT.Abs).then_inc(z_abs, 1)
                act.wait_ge(z_abs, j + 2)
                nc.scalar.activation(e_first[:, j:j + 2, :], e_first[:, j:j + 2, :], ACT.Exp, scale=-1.0).then_inc(e_set, 2)
            act.sem_inc(w_set, KC)
            for j in range(0, KC, 2):
                act.wait_ge(e_set, j + 2)
                nc.scalar.activation(l_first[:, j:j + 2, :], e_first[:, j:j + 2, :], ACT.Ln, bias=1.0).then_inc(ln_set, 2)
            take_c(0)
            act.wait_ge(al_in, 16)
            nc.scalar.activation(A[:], A[:], ACT.Exp).then_inc(A_exp, 1)
            act.wait_ge(A_set, 1)
            act.wait_ge(zero_set, 1)
            round_0()
            round_(1, last2=False)
            with act.Fori(2, BATCH - 1) as r:
                round_(r)
            round_(BATCH - 1, setup=False)
            round_(BATCH, scans=False, setup=False)
            norm2(BATCH, 2)
            norm2(BATCH, 3)
            act.wait_ge(out_done, 64 * BATCH)

        @block.gpsimd
        def _(pool):
            def b_slot(r, s, par, lane, fourth):
                pool.wait_ge(b_in[lane], 64 * r + 16 * fourth + 16)
                wait(pool, scan_done, 16 * r + s - 1)
                nc.gpsimd.tensor_tensor(dBx[:, par, :, :], u_chan[:],
                                        Bb[:, lane:lane + 1, :].to_broadcast([P, KC, SEQ]), ALU.mult).then_inc(dBx_ready, 1)

            def static_slot(r, s):
                b_slot(r, s, s % 2, s % 4, s // 4)

            def take_row(r):
                pool.wait_ge(dt_set, 4 * r + 4)
                wait(pool, dBx_ready, 16 * r)
                nc.gpsimd.tensor_tensor(u_chan[:], dt_next[:], x_chan[:], ALU.mult).then_inc(u_set, 1)
                pool.wait_ge(u_set, r + 1)

            def rstd1(r):
                for j in range(2):
                    pool.wait_ge(ln1_ve, 2 * r - 1 + j)
                    nc.gpsimd.tensor_tensor(rstd[:, 2 * j:2 * j + 2], mv[:, 2 * j:2 * j + 2, 1], neg_half[:, 0:2], ALU.pow
                                            ).then_inc(ln1_rstd, 1)

            def rstd_2(r, c):
                pool.wait_ge(ln2_ve, 4 * (r - 1) + c + 1)
                nc.gpsimd.tensor_tensor(rstd2[:, c:c + 1], ve2[:, c:c + 1], neg_half[:, 0:1], ALU.pow).then_inc(ln2_rstd, 1)
                pool.wait_ge(ln2_rstd, 4 * (r - 1) + c + 1)
                nc.gpsimd.tensor_tensor(nmr2[:, c:c + 1], nm2[:, c:c + 1], rstd2[:, c:c + 1], ALU.mult).then_inc(ln2_nmr, 1)

            def low_h(r, t):
                for q in range(2):
                    pool.wait_ge(hh_set, OT * (r - 1) + t + (q + 1))
                    nc.gpsimd.tensor_tensor(hp[:, 1, ds(t + q, 1), :].rearrange("p a t -> p (a t)"), sh[:, 2 + q, :],
                                            hp[:, 0, ds(t + q, 1), :].rearrange("p a t -> p (a t)"),
                                            ALU.subtract).then_inc(hl_set, 1)

            def softplus_lost(b, k):
                n = 4 * b + k + 1
                pool.wait_ge(w1_set, n)
                nc.gpsimd.tensor_tensor(t_sp[k % 2], e_sp[k % 2], t_sp[k % 2], ALU.subtract).then_inc(r_set, 1)

            def scale_x(r):
                pool.wait_ge(x_in, 16 * r + 16)
                nc.gpsimd.tensor_tensor(x_tok[:], x_tok[:], D1[:].rearrange("p (a d) -> p a d", a=1).to_broadcast([P, TC, D]),
                                        ALU.mult).then_inc(xd_set, 1)

            def round_(r, scans=True, ffn=True, last2=True, setup=True):
                if is_first(r):
                    pool.wait_ge(dt_set, 2)
                    for k in (0, 1):
                        pool.wait_ge(x_first_in[k], 16)
                    nc.gpsimd.tensor_tensor(u_chan[:, 0:2, :], dt_chan[:, 0:2, :], x_chan[:, 0:2, :], ALU.mult
                                            ).then_inc(u_set, 1)
                    pool.wait_ge(u_set, 1)
                    pool.wait_ge(b_in[0], 16)
                    nc.gpsimd.tensor_tensor(dBx[:, 0, 0:2, :], u_chan[:, 0:2, :],
                                            Bb[:, 0:1, :].to_broadcast([P, 2, SEQ]), ALU.mult).then_inc(dBx_half, 1)
                    pool.wait_ge(u_half, 1)
                    pool.wait_ge(dBx_ready, 1)
                elif scans:
                    take_row(r)
                    static_slot(r, 0)
                if last2:
                    rstd_2(r - 1, 2)
                if scans:
                    static_slot(r, 1)
                if last2:
                    rstd_2(r - 1, 3)
                if scans and ffn:
                    scale_x(r)
                if ffn:
                    rstd1(r)
                if scans:
                    static_slot(r, 2)
                with pool.Fori(0, 2) as i:
                    for n in range(4):
                        if scans:
                            b_slot(r, 4 * i + (3 + n), (1 + n) % 2, (3 + n) % 4, i + (3 + n) // 4)
                        if ffn and n < 3:
                            low_h(r, 6 * i + 2 * n)
                if scans:
                    static_slot(r, 11)
                if ffn:
                    low_h(r, 12)
                for s in range(11, NS):
                    if scans and s > 11:
                        static_slot(r, s)
                    if setup and s in (11, 13):
                        softplus_lost(r + 1, s - 11)
                        softplus_lost(r + 1, s - 10)
                    if ffn and s in DONE_BY:
                        rstd_2(r, DONE_BY.index(s))

            nc.gpsimd.memset(dA[:], 0.0).then_inc(zero_set, 1)
            nc.gpsimd.memset(neg_half[:], -0.5).then_inc(nh_set, 1)
            pool.sem_inc(hl_set, 2)
            pool.wait_ge(nh_set, 1)
            pool.wait_ge(c_par, 1)
            nc.gpsimd.partition_all_reduce(small[:, 1:2], small[:, 0:1], P, bass.bass_isa.ReduceOp.max).then_inc(c_all, 1)
            pool.wait_ge(c_all, 1)
            nc.gpsimd.tensor_tensor(small[:, 2:3], small[:, 1:2], neg_half[:, 0:1], ALU.pow).then_inc(c_pow, 1)
            round_(0, ffn=False, last2=False)
            round_(1, last2=False)
            with pool.Fori(2, BATCH - 1) as r:
                round_(r)
            round_(BATCH - 1, setup=False)
            round_(BATCH, scans=False, setup=False)
            rstd_2(BATCH, 2)
            rstd_2(BATCH, 3)

        @block.vector
        def _(dve):
            def scan(r, s, par):
                dve.wait_ge(dBx_ready, 16 * r + s + 1)
                dve.wait_ge(dA_ready, 64 * r + 4 * s + 4)
                wait(dve, H_done, 64 * r + 4 * s - 4)
                nc.vector.tensor_tensor_scan(h[:, par, :, :].rearrange("p k t -> p (k t)"),
                                             dA[:, par, :, :].rearrange("p k t -> p (k t)"),
                                             dBx[:, par, :, :].rearrange("p k t -> p (k t)"), 0.0,
                                             ALU.mult, ALU.add).then_inc(scan_done, 1)

            def add(r, s, c, n):
                dve.wait_ge(H_done, 64 * r + 4 * s - 3 + c)
                wait(dve, acc_done, 64 * r + 4 * s - 7 + c)
                before = x_tok if isinstance(n, int) and n == 0 else acc
                nc.vector.scalar_tensor_tensor(acc[:, c, :], bank(r, c), C_cur[:, c, ds(n, 1)], before[:, c, :],
                                               ALU.mult, ALU.add).then_inc(acc_done, 1)

            def slot(r, s, par, scans=True, between=(), scan_at=0):
                for c in range(TC + 1):
                    if scans and c == scan_at:
                        scan(r, s, par)
                    for piece in (between[c] if c < len(between) else ()):
                        piece()
                    if scans and c < TC:
                        add(r, s, c, s - 1)

            def ln1_stats(r, c):
                dve.wait_ge(acc_done, 64 * r - 3 + c)
                apart(dve)
                nc.vector.bn_stats(st[:, c, :], acc[:, c, :]).then_inc(ln1_st, 1)

            def ln1_var(r, j):
                dve.wait_ge(ln1_st, 4 * r - 2 + 2 * j)
                apart(dve)
                for c in (2 * j, 2 * j + 1):
                    last = nc.vector.bn_aggr(mv[:, c, :], st[:, c, :])
                last.then_inc(ln1_mv, 1)
                dve.wait_ge(ln1_mv, 2 * r - 1 + j)
                nc.vector.tensor_scalar(mv[:, 2 * j:2 * j + 2, 1], mv[:, 2 * j:2 * j + 2, 1], EPS, None, ALU.add
                                        ).then_inc(ln1_ve, 1)

            def ln1(r):
                if not isinstance(r, int) or r > 1:
                    dve.wait_ge(y_set, 4 * r - 4)
                for c in range(TC):
                    if c % 2 == 0:
                        dve.wait_ge(ln1_rstd, 2 * r - 1 + c // 2)
                    nc.vector.tensor_scalar(x2[:, c, :], acc[:, c, :], mv[:, c, 0:1], rstd[:, c:c + 1],
                                            ALU.subtract, ALU.mult).then_inc(x2_set, 1)

            def take_C(r):
                dve.wait_ge(cn_set, r + 1)
                nc.vector.tensor_copy(C_cur[:], C_next[:]).then_inc(C_set, 1)
                dve.wait_ge(C_set, r + 1)
                dve.wait_ge(xd_set, r + 1)

            def softplus_sum(b, k):
                n = 4 * b + k + 1
                dve.wait_ge(ln_set, n)
                nc.vector.tensor_tensor(t_sp[k % 2], t_sp[k % 2], e_sp[k % 2], ALU.add).then_inc(l_set, 1)
                dve.wait_ge(l_set, n)
                nc.vector.scalar_tensor_tensor(dt_next[:, k, :], G[k % 2][:], 0.0, t_sp[k % 2], ALU.max, ALU.add
                                               ).then_inc(dt_set, 1)

            def low_x(r):
                for k in range(KC):
                    dve.wait_ge(xh_set, 4 * (r - 1) + k + 1)
                    nc.vector.scalar_tensor_tensor(xl[:, k, :], F[:, k, :], X_UP, xh[:, k, :],
                                                   ALU.mult, ALU.subtract).then_inc(xl_set, 1)

            def tiles(r, t, qs=range(2)):
                for q in qs:
                    dve.wait_ge(up_ps, OT * (r - 1) + t + (q + 1))
                    dve.wait_ge(silu_set, OT * (r - 1) + t + (q + 1))
                    dve.wait_ge(hl_set, OT * (r - 1) + t + (q + 1))
                    nc.vector.scalar_tensor_tensor(sh[:, 2 + q, :], F[:, 2 + q, :], us_sb[:, ds(t + q, 1)], sh[:, q, :],
                                                   ALU.mult, ALU.mult).then_inc(h_set, 1)

            def finish(r, c, setup):
                n = 4 * (r - 1) + c + 1

                def scaled():
                    dve.wait_ge(down_ps, n)
                    if not isinstance(r, int) or r > 1:
                        dve.wait_ge(out_done, 64 * r - 64)
                    if setup and c == 2:
                        dve.wait_ge(b_out, 16 * r + 32)
                        dve.wait_ge(cn_set, r + 2)
                    if setup and c == 3:
                        dve.wait_ge(z_ps, 4 * r + 8)
                    nc.vector.tensor_tensor(ybuf[:, c, :], F[:, c, :], ds_bc[:], ALU.mult).then_inc(ds_done, 1)

                def plus_x2():
                    dve.wait_ge(ds_done, n)
                    nc.vector.tensor_tensor(ybuf[:, c, :], ybuf[:, c, :], x2[:, c, :], ALU.add).then_inc(y_set, 1)

                def stats():
                    dve.wait_ge(y_set, n)
                    apart(dve)
                    nc.vector.bn_stats(st2[:, c, :], ybuf[:, c, :]).then_inc(ln2_st, 1)

                def mean_var():
                    dve.wait_ge(ln2_st, n)
                    apart(dve)
                    nc.vector.bn_aggr(mv2[:, c, :], st2[:, c, :]).then_inc(ln2_mv, 1)
                    dve.wait_ge(ln2_mv, n)
                    nc.vector.tensor_scalar(nm2[:, c:c + 1], mv2[:, c, 0:1], -1.0, None, ALU.mult)
                    nc.vector.tensor_scalar(ve2[:, c:c + 1], mv2[:, c, 1:2], EPS, None, ALU.add).then_inc(ln2_ve, 1)
                    dve.wait_ge(ln2_ve, n)

                return scaled, plus_x2, stats, mean_var

            def round_(r, scans=True, ffn=True, setup=True):
                if scans:
                    scan(r, 0, 0)
                if ffn:
                    for c in range(TC):
                        add(r, 0, c, NS - 1)
                        if c > 0:
                            ln1_stats(r, c - 1)
                        if c == 2:
                            ln1_var(r, 0)
                    ln1_stats(r, TC - 1)
                    ln1_var(r, 1)
                if ffn:
                    ln1(r)
                    dve.wait_ge(x2_set, 4 * r)
                if scans:
                    take_C(r)
                    add(r, 1, 0, 0)
                    add(r, 1, 1, 0)
                if ffn:
                    low_x(r)
                if scans:
                    scan(r, 1, 1)
                    add(r, 1, 2, 0)
                    add(r, 1, 3, 0)
                if ffn:
                    if scans:
                        dve.wait_ge(u_set, r + 1)
                        dve.wait_ge(dt_cur, r + 1)
                        apart(dve)
                with dve.Fori(0, 2) as i:
                    for n in range(4):
                        halves = [[lambda q=q, n=n: tiles(r, 6 * i + 2 * n, qs=(q,))] for q in range(2)] if ffn and n < 3 else []
                        slot(r, 4 * i + (2 + n), n % 2, scans, [[]] * min(n, 2) + halves)
                for s in range(10, NS):
                    between = [[], [], [], [], []]
                    if ffn and s == 10:
                        between[0].append(lambda: tiles(r, 12, qs=(0,)))
                        between[1].append(lambda: tiles(r, 12, qs=(1,)))
                    if setup:
                        for k, at in enumerate(SUM_AT):
                            if s == at[0]:
                                between[at[1]].append(lambda k=k: softplus_sum(r + 1, k))
                    if ffn:
                        for c, at in enumerate(DOWN_BY):
                            if s == at:
                                for j, piece in enumerate(finish(r, c, setup)):
                                    between[min(j + 1, 4)].append(piece)
                    slot(r, s, s % 2, scans, between, scan_at=1 if ffn else 0)

            dve.sem_inc(h_set, 2)
            dve.wait_ge(scale_in, 64)
            nc.vector.tensor_scalar(D1[:], D1[:], 1.0, None, ALU.add).then_inc(D1_set, 1)
            dve.wait_ge(D1_set, 1)
            dve.wait_ge(x_in, 16)
            nc.vector.tensor_tensor(x_tok[:], x_tok[:], D1[:].rearrange("p (a d) -> p a d", a=1).to_broadcast([P, TC, D]),
                                    ALU.mult).then_inc(xd_set, 1)
            nc.vector.tensor_tensor(gu[:], gs_sb[:], us_sb[:], ALU.mult).then_inc(c_gu, 1)
            dve.wait_ge(c_gu, 1)
            nc.vector.tensor_tensor(gu[:], gu[:], gu[:], ALU.mult).then_inc(c_sq, 1)
            dve.wait_ge(c_sq, 1)
            nc.vector.reduce_max(small[:, 0:1], gu[:], mybir.AxisListType.X).then_inc(c_max, 1)
            dve.wait_ge(c_max, 1)
            nc.vector.tensor_scalar(small[:, 0:1], small[:, 0:1], 1e-30, None, ALU.max).then_inc(c_par, 1)
            for j in range(0, KC, 2):
                dve.wait_ge(e_set, j + 2)
                nc.vector.tensor_scalar(t_first[:, j:j + 2, :], e_first[:, j:j + 2, :], 1.0, -1.0, ALU.add, ALU.add
                                        ).then_inc(w1_set, 2)
                dve.wait_ge(w1_set, j + 2)
                nc.vector.tensor_tensor(t_first[:, j:j + 2, :], e_first[:, j:j + 2, :], t_first[:, j:j + 2, :], ALU.subtract
                                        ).then_inc(r_set, 2)
            for j in range(0, KC, 2):
                dve.wait_ge(ln_set, j + 2)
                dve.wait_ge(r_set, j + 2)
                nc.vector.tensor_tensor(t_first[:, j:j + 2, :], t_first[:, j:j + 2, :], l_first[:, j:j + 2, :], ALU.add
                                        ).then_inc(l_set, 2)
                dve.wait_ge(l_set, j + 2)
                for k in (j, j + 1):
                    nc.vector.scalar_tensor_tensor(dt_chan[:, k, :], F[:, k, :], 0.0, t_first[:, k, :], ALU.max, ALU.add
                                                   ).then_inc(dt_set, 1)
            dve.wait_ge(A_exp, 1)
            nc.vector.tensor_scalar(A[:], A[:], -1.0, None, ALU.mult).then_inc(A_set, 1)
            dve.wait_ge(dt_set, KC)
            for k in (2, 3):
                dve.wait_ge(x_first_in[k], 16)
            nc.vector.tensor_tensor(u_chan[:, 2:4, :], dt_chan[:, 2:4, :], x_chan[:, 2:4, :], ALU.mult).then_inc(u_half, 1)
            dve.wait_ge(u_half, 1)
            dve.wait_ge(b_in[0], 16)
            dve.wait_ge(dBx_half, 1)
            nc.vector.tensor_tensor(dBx[:, 0, 2:4, :], u_chan[:, 2:4, :], Bb[:, 0:1, :].to_broadcast([P, 2, SEQ]), ALU.mult
                                    ).then_inc(dBx_ready, 1)
            round_(0, ffn=False)
            dve.wait_ge(c_pow, 1)
            nc.vector.tensor_scalar(small[:, 3:4], small[:, 2:3], H_TOP / H_BOUND, None, ALU.mult).then_inc(c_set, 1)
            dve.wait_ge(c_set, 1)
            nc.vector.reciprocal(small[:, 4:5], small[:, 3:4]).then_inc(c_inv, 1)
            dve.wait_ge(c_inv, 1)
            nc.vector.tensor_scalar(ds_bc[:], ds_bc[:], small[:, 4:5], None, ALU.mult)
            nc.vector.tensor_scalar(us_sb[:], us_sb[:], small[:, 3:4], 1.0 / X_UP, ALU.mult, ALU.mult)
            nc.vector.tensor_scalar(gs_sb[:], gs_sb[:], 1.0 / X_UP, None, ALU.mult).then_inc(scales_set, 1)
            dve.wait_ge(scales_set, 1)
            with dve.Fori(1, BATCH - 1) as r:
                round_(r)
            round_(BATCH - 1, setup=False)
            round_(BATCH, scans=False, setup=False)


def kernel(**inputs):
    import numpy as np
    import concourse.bacc as bacc
    from concourse.bass_utils import run_bass_kernel_spmd

    a = {k.replace("L0_attn_", "").replace("L0_ffn_", ""): np.asarray(val) for k, val in inputs.items()}

    def t_(w):
        return np.ascontiguousarray(w.T)

    arrays = {
        "x": np.ascontiguousarray(a["x"]),
        "x_chan": np.ascontiguousarray(a["x"].transpose(0, 2, 1)),
        "A_log": np.ascontiguousarray(a["A_log"]),
        "Dw": a["D"].reshape(1, -1),
        "xproj": t_(np.concatenate([a["x_proj_w"][:RK], a["x_proj_w"][RK + NS:], a["x_proj_w"][RK:RK + NS]])),
        "dtw": t_(a["dt_proj_w"]),
        "dt_b": a["dt_proj_b"].reshape(1, -1),
        "wg": t_(a["gate_wq"]),
        "gs": t_(a["gate_scale"].reshape(-1, 128)),
        "wu": t_(a["up_wq"]),
        "us": t_(a["up_scale"].reshape(-1, 128)),
        "wd": t_(a["down_wq"]),
        "dscale": a["down_scale"].reshape(1, -1),
        "identity": np.eye(128, dtype=np.float32),
    }
    nc = bacc.Bacc("TRN2", target_bir_lowering=False, num_devices=1)
    args = [nc.dram_tensor(f"in_{n}", v.shape, mybir.dt.from_np(v.dtype), kind="ExternalInput").ap()
            for n, v in arrays.items()]
    out = nc.dram_tensor("out_y", (BATCH * SEQ, D), fp32, kind="ExternalOutput").ap()
    build(nc, *args, out)
    r = run_bass_kernel_spmd(nc, [{f"in_{n}": v for n, v in arrays.items()}], core_ids=[0])
    return r.results[0]["out_y"].reshape(BATCH, SEQ, D)
```
